# Optimizing a Trainium2 kernel written in Bass

```python
import numpy as np
import jax
import jax.numpy as jnp

def _softmax(x, axis=-1):
    return jax.nn.softmax(x, axis=axis)

def _gelu(x):
    return jax.nn.gelu(x, approximate=True)

def _silu(x):
    return jax.nn.silu(x)

def _sigmoid(x):
    return jax.nn.sigmoid(x)

def _layernorm(x, axis=-1, eps=1e-05):
    m = jnp.mean(x, axis=axis, keepdims=True)
    v = jnp.var(x, axis=axis, keepdims=True)
    return (x - m) / jnp.sqrt(v + eps)

def _scatter_add(tgt, idx, src, axis=0):
    return tgt.at[idx].add(src)

def _segment_sum(src, seg, n):
    return jax.ops.segment_sum(src, seg, n)
kernel_name = 'mk_adaln_attn_ffn_d1_seqx_r8_7aa033'

def setup_inputs(seed: int=0):
    np.random.seed(seed)
    _w = jnp.asarray

    def _rec_inputs():
        import jax
        import jax.numpy as jnp
        _rk = jax.random.key(seed)
        x = 4.136e-05 + 0.9999 * jax.random.normal(jax.random.fold_in(_rk, 1), (4, 256, 128), jnp.float32)
        _lenS = 256 - jax.random.randint(jax.random.fold_in(_rk, 7), (4,), 0, max(1, 256 // 4) + 1, jnp.int32)
        _lenS2 = 256 - jax.random.randint(jax.random.fold_in(_rk, 8), (4,), 0, max(1, 256 // 4) + 1, jnp.int32)
        cond_1024 = -0.00608245 + 1.00131 * jax.random.normal(jax.random.fold_in(_rk, 11), (4, 128), jnp.float32)
        return (x, cond_1024)
    x, cond_1024 = _rec_inputs()

    def _L0_cond_setup():
        import jax, jax.numpy as jnp
        import numpy as np
        B, T, D_IN, V_IN, E = (64, 128, 128, 128, 128)
        key = jax.random.key(seed)
        ks = jax.random.split(key, 16)
        s = 0.01
        return {'video': jax.random.normal(ks[0], (B, V_IN), jnp.float32), 'seq': jax.random.normal(ks[1], (B, T, D_IN), jnp.float32), 'W_z': jax.random.normal(ks[2], (D_IN, E), jnp.float32) * s, 'U_z': jax.random.normal(ks[3], (E, E), jnp.float32) * s, 'C_z': jax.random.normal(ks[4], (V_IN, E), jnp.float32) * s, 'b_z': jnp.zeros((E,), jnp.float32), 'W_r': jax.random.normal(ks[5], (D_IN, E), jnp.float32) * s, 'U_r': jax.random.normal(ks[6], (E, E), jnp.float32) * s, 'C_r': jax.random.normal(ks[7], (V_IN, E), jnp.float32) * s, 'b_r': jnp.zeros((E,), jnp.float32), 'W': jax.random.normal(ks[8], (D_IN, E), jnp.float32) * s, 'U': jax.random.normal(ks[9], (E, E), jnp.float32) * s, 'C': jax.random.normal(ks[10], (V_IN, E), jnp.float32) * s, 'b': jnp.zeros((E,), jnp.float32)}
    _L0_cond_all = _L0_cond_setup()
    _L0_cond_in = {k: v for k, v in _L0_cond_all.items() if k in ('W_z', 'U_z', 'C_z', 'b_z', 'W_r', 'U_r', 'C_r', 'b_r', 'W', 'U', 'C', 'b')}
    del _L0_cond_all

    def _L0_attn_setup():
        import jax, jax.numpy as jnp
        import numpy as np
        B, T, C = (4, 512, 128)
        key = jax.random.key(seed)
        x = jax.random.normal(key, (B, T, C), dtype=jnp.float32)
        return {'x': x}
    _L0_attn_all = _L0_attn_setup()
    _L0_attn_in = {k: v for k, v in _L0_attn_all.items() if k in ()}
    del _L0_attn_all

    def _L0_cond2_setup():
        import jax, jax.numpy as jnp
        import numpy as np
        D, HS, HE, E, K = (128, 256, 128, 8, 2)
        B, T = (4, 128)
        N_SHARED = 1
        key = jax.random.key(seed)
        ks = jax.random.split(key, 9)
        g = lambda k, shape, s: jax.random.normal(k, shape, jnp.float32) * s
        return {'x': g(ks[0], (B, T, D), 1.0), 't_emb': g(ks[1], (B, D), 1.0), 'router_W': g(ks[2], (2 * D, E), 0.01), 'router_bias': jnp.zeros((E,), jnp.float32), 'w1': g(ks[3], (D, HS), 0.02), 'w3': g(ks[4], (D, HS), 0.02), 'w2': g(ks[5], (HS, D), 0.02), 'W1e': g(ks[6], (E, D, HE), 0.02), 'W2e': g(ks[7], (E, HE, D), 0.02)}
    _L0_cond2_all = _L0_cond2_setup()
    _L0_cond2_in = {k: v for k, v in _L0_cond2_all.items() if k in ('router_W', 'router_bias', 'w1', 'w3', 'w2', 'W1e', 'W2e')}
    del _L0_cond2_all

    def _L0_ffn_setup():
        import jax, jax.numpy as jnp
        import numpy as np
        DIM = 128
        HEADS = 16
        HD = DIM // HEADS
        M = 32
        E = 4
        K = 2
        HID = 256
        MID = 256
        LB = 0.01
        EPS = 1.1920929e-07

        def _rms(x, w):
            return x * jax.lax.rsqrt(jnp.mean(x * x, axis=-1, keepdims=True) + EPS) * w

        def _gelu(x):
            return jax.nn.gelu(x, approximate=False)
        key = jax.random.key(seed)
        ks = jax.random.split(key, 20)
        d = DIM
        w = lambda k, s: jax.random.normal(k, s, jnp.float32) * 0.02
        return {'x': jax.random.normal(ks[0], (4, 128, d), jnp.float32), 'n1_w': jnp.ones((d,), jnp.float32), 'n2_w': jnp.ones((d,), jnp.float32), 'wq': w(ks[1], (d, d)), 'wk': w(ks[2], (d, d)), 'wv': w(ks[3], (d, d)), 'wo': w(ks[4], (d, d)), 'qn_w': jnp.ones((HD,), jnp.float32), 'kn_w': jnp.ones((HD,), jnp.float32), 'gate_w': w(ks[5], (E, d)), 'e0_up': w(ks[6], (HID, d)), 'e0_down': w(ks[7], (d, HID)), 'e1_w1': w(ks[8], (HID, d)), 'e1_w2': w(ks[9], (HID, d)), 'e1_down': w(ks[10], (d, HID)), 'e2_l1': w(ks[11], (MID, d)), 'e2_l2': w(ks[12], (HID, MID)), 'e2_l3': w(ks[13], (MID, HID)), 'e2_l4': w(ks[14], (d, MID)), 'e3_down': w(ks[15], (d, d)), 'e3_up': w(ks[16], (HID, d)), 'e3_out': w(ks[17], (d, HID))}
    _L0_ffn_all = _L0_ffn_setup()
    _L0_ffn_in = {k: v for k, v in _L0_ffn_all.items() if k in ('n1_w', 'n2_w', 'wq', 'wk', 'wv', 'wo', 'qn_w', 'kn_w', 'gate_w', 'e0_up', 'e0_down', 'e1_w1', 'e1_w2', 'e1_down', 'e2_l1', 'e2_l2', 'e2_l3', 'e2_l4', 'e3_down', 'e3_up', 'e3_out')}
    del _L0_ffn_all
    return {'x': x, 'cond_1024': cond_1024, 'L0_cond_W_z': _L0_cond_in['W_z'], 'L0_cond_U_z': _L0_cond_in['U_z'], 'L0_cond_C_z': _L0_cond_in['C_z'], 'L0_cond_b_z': _L0_cond_in['b_z'], 'L0_cond_W_r': _L0_cond_in['W_r'], 'L0_cond_U_r': _L0_cond_in['U_r'], 'L0_cond_C_r': _L0_cond_in['C_r'], 'L0_cond_b_r': _L0_cond_in['b_r'], 'L0_cond_W': _L0_cond_in['W'], 'L0_cond_U': _L0_cond_in['U'], 'L0_cond_C': _L0_cond_in['C'], 'L0_cond_b': _L0_cond_in['b'], 'L0_cond2_router_W': _L0_cond2_in['router_W'], 'L0_cond2_router_bias': _L0_cond2_in['router_bias'], 'L0_cond2_w1': _L0_cond2_in['w1'], 'L0_cond2_w3': _L0_cond2_in['w3'], 'L0_cond2_w2': _L0_cond2_in['w2'], 'L0_cond2_W1e': _L0_cond2_in['W1e'], 'L0_cond2_W2e': _L0_cond2_in['W2e'], 'L0_ffn_n1_w': _L0_ffn_in['n1_w'], 'L0_ffn_n2_w': _L0_ffn_in['n2_w'], 'L0_ffn_wq': _L0_ffn_in['wq'], 'L0_ffn_wk': _L0_ffn_in['wk'], 'L0_ffn_wv': _L0_ffn_in['wv'], 'L0_ffn_wo': _L0_ffn_in['wo'], 'L0_ffn_qn_w': _L0_ffn_in['qn_w'], 'L0_ffn_kn_w': _L0_ffn_in['kn_w'], 'L0_ffn_gate_w': _L0_ffn_in['gate_w'], 'L0_ffn_e0_up': _L0_ffn_in['e0_up'], 'L0_ffn_e0_down': _L0_ffn_in['e0_down'], 'L0_ffn_e1_w1': _L0_ffn_in['e1_w1'], 'L0_ffn_e1_w2': _L0_ffn_in['e1_w2'], 'L0_ffn_e1_down': _L0_ffn_in['e1_down'], 'L0_ffn_e2_l1': _L0_ffn_in['e2_l1'], 'L0_ffn_e2_l2': _L0_ffn_in['e2_l2'], 'L0_ffn_e2_l3': _L0_ffn_in['e2_l3'], 'L0_ffn_e2_l4': _L0_ffn_in['e2_l4'], 'L0_ffn_e3_down': _L0_ffn_in['e3_down'], 'L0_ffn_e3_up': _L0_ffn_in['e3_up'], 'L0_ffn_e3_out': _L0_ffn_in['e3_out']}

def reference(x, cond_1024, L0_cond_W_z, L0_cond_U_z, L0_cond_C_z, L0_cond_b_z, L0_cond_W_r, L0_cond_U_r, L0_cond_C_r, L0_cond_b_r, L0_cond_W, L0_cond_U, L0_cond_C, L0_cond_b, L0_cond2_router_W, L0_cond2_router_bias, L0_cond2_w1, L0_cond2_w3, L0_cond2_w2, L0_cond2_W1e, L0_cond2_W2e, L0_ffn_n1_w, L0_ffn_n2_w, L0_ffn_wq, L0_ffn_wk, L0_ffn_wv, L0_ffn_wo, L0_ffn_qn_w, L0_ffn_kn_w, L0_ffn_gate_w, L0_ffn_e0_up, L0_ffn_e0_down, L0_ffn_e1_w1, L0_ffn_e1_w2, L0_ffn_e1_down, L0_ffn_e2_l1, L0_ffn_e2_l2, L0_ffn_e2_l3, L0_ffn_e2_l4, L0_ffn_e3_down, L0_ffn_e3_up, L0_ffn_e3_out):
    import jax
    import jax.numpy as jnp

    def _L0_cond_ref(video, seq, W_z, U_z, C_z, b_z, W_r, U_r, C_r, b_r, W, U, C, b):
        import jax, jax.numpy as jnp
        import numpy as np
        B, T, D_IN, V_IN, E = (64, 128, 128, 128, 128)
        vz = video @ C_z + b_z
        vr = video @ C_r + b_r
        vh = video @ C + b
        xz = jnp.einsum('btd,de->bte', seq, W_z)
        xr = jnp.einsum('btd,de->bte', seq, W_r)
        xh = jnp.einsum('btd,de->bte', seq, W)

        def step(h, xs):
            xzt, xrt, xht = xs
            z = jax.nn.sigmoid(xzt + h @ U_z + vz)
            r = jax.nn.sigmoid(xrt + h @ U_r + vr)
            hh = jnp.tanh(xht + r * h @ U + vh)
            h_new = (1.0 - z) * h + z * hh
            return (h_new, h_new)
        h0 = jnp.zeros((seq.shape[0], U.shape[0]), seq.dtype)
        xs = (jnp.swapaxes(xz, 0, 1), jnp.swapaxes(xr, 0, 1), jnp.swapaxes(xh, 0, 1))
        _, out_t = jax.lax.scan(step, h0, xs)
        return jnp.swapaxes(out_t, 0, 1)

    def _L0_attn_ref(x):
        import jax, jax.numpy as jnp
        import numpy as np
        B, T, C = (4, 512, 128)
        t = x.shape[1]
        tril = jnp.tril(jnp.ones((t, t), dtype=x.dtype))
        wei = jnp.where(tril == 0, -jnp.inf, jnp.zeros((t, t), dtype=x.dtype))
        wei = jax.nn.softmax(wei, axis=-1)
        out = jnp.einsum('ts,bsc->btc', wei, x)
        return out

    def _L0_cond2_ref(x, t_emb, router_W, router_bias, w1, w3, w2, W1e, W2e):
        import jax, jax.numpy as jnp
        import numpy as np
        D, HS, HE, E, K = (128, 256, 128, 8, 2)
        B, T = (4, 128)
        N_SHARED = 1
        Bb, Tt, C = x.shape
        xf = x.reshape(-1, C)
        tf = jnp.broadcast_to(t_emb[:, None, :], (Bb, Tt, C)).reshape(-1, C)
        N = xf.shape[0]
        shared = jax.nn.silu(xf @ w1) * (xf @ w3) @ w2
        s = jax.nn.sigmoid((jnp.concatenate([xf, tf], axis=-1) @ router_W).astype(jnp.float32))
        sel_scores = s + router_bias
        _, topk_idx = jax.lax.top_k(sel_scores, K)
        s_sel = jnp.take_along_axis(s, topk_idx, axis=1)
        denom = s_sel.sum(axis=1, keepdims=True)
        gates = jnp.where(denom > 1e-09, s_sel / (denom + 1e-09), 1.0 / K).astype(x.dtype)
        combine = jnp.zeros((N, E), x.dtype).at[jnp.arange(N)[:, None], topk_idx].add(gates)
        h = jax.nn.gelu(jnp.einsum('nc,ech->enh', xf, W1e), approximate=False)
        y = jnp.einsum('enh,ehc->enc', h, W2e)
        routed = jnp.einsum('ne,enc->nc', combine, y)
        return ((shared + routed) / (N_SHARED + K)).reshape(Bb, Tt, C)

    def _L0_ffn_ref(x, n1_w, n2_w, wq, wk, wv, wo, qn_w, kn_w, gate_w, e0_up, e0_down, e1_w1, e1_w2, e1_down, e2_l1, e2_l2, e2_l3, e2_l4, e3_down, e3_up, e3_out):
        import jax, jax.numpy as jnp
        import numpy as np
        DIM = 128
        HEADS = 16
        HD = DIM // HEADS
        M = 32
        E = 4
        K = 2
        HID = 256
        MID = 256
        LB = 0.01
        EPS = 1.1920929e-07

        def _rms(x, w):
            return x * jax.lax.rsqrt(jnp.mean(x * x, axis=-1, keepdims=True) + EPS) * w

        def _gelu(x):
            return jax.nn.gelu(x, approximate=False)
        B, T, C = x.shape
        h = _rms(x, n1_w)
        heads = lambda w_: (h @ w_.T).reshape(B, T, HEADS, HD).transpose(0, 2, 1, 3)
        q = _rms(heads(wq), qn_w)
        k = _rms(heads(wk), kn_w)
        v = heads(wv)
        scores = jnp.einsum('bhqd,bhkd->bhqk', q, k) * HD ** (-0.5)
        causal = jnp.tril(jnp.ones((T, T), bool))
        scores = jnp.where(causal[None, None], scores, -jnp.inf)
        attn = jax.nn.softmax(scores, axis=-1)
        ao = jnp.einsum('bhqk,bhkd->bhqd', attn, v).transpose(0, 2, 1, 3).reshape(B, T, C) @ wo.T
        ao = ao.at[:, :, :M].set(0.0)
        x = x + ao
        xf = _rms(x, n2_w).reshape(-1, C)
        N = xf.shape[0]
        logits = jnp.nan_to_num(xf @ gate_w.T)
        probs = jax.nn.softmax(logits, axis=-1)
        topv, topi = jax.lax.top_k(probs, K)
        topv = topv / (topv.sum(-1, keepdims=True) + 1e-08)
        wts = jnp.zeros((N, E), x.dtype).at[jnp.arange(N)[:, None], topi].add(topv)
        o0 = _gelu(xf @ e0_up.T) @ e0_down.T
        o1 = jax.nn.silu(xf @ e1_w1.T) * (xf @ e1_w2.T) @ e1_down.T
        o2 = _gelu(_gelu(_gelu(xf @ e2_l1.T) @ e2_l2.T) @ e2_l3.T) @ e2_l4.T
        o3 = _gelu(_gelu(xf @ e3_down.T) @ e3_up.T) @ e3_out.T
        moe = wts[:, 0:1] * o0 + wts[:, 1:2] * o1 + wts[:, 2:3] * o2 + wts[:, 3:4] * o3
        moe = moe.reshape(B, T, C).at[:, :, :M].set(0.0)
        return x + moe
    x = x + _L0_attn_ref(_L0_cond_ref(cond_1024, x, L0_cond_W_z, L0_cond_U_z, L0_cond_C_z, L0_cond_b_z, L0_cond_W_r, L0_cond_U_r, L0_cond_C_r, L0_cond_b_r, L0_cond_W, L0_cond_U, L0_cond_C, L0_cond_b))
    x = x + _L0_ffn_ref(_L0_cond2_ref(x, cond_1024, L0_cond2_router_W, L0_cond2_router_bias, L0_cond2_w1, L0_cond2_w3, L0_cond2_w2, L0_cond2_W1e, L0_cond2_W2e), L0_ffn_n1_w, L0_ffn_n2_w, L0_ffn_wq, L0_ffn_wk, L0_ffn_wv, L0_ffn_wo, L0_ffn_qn_w, L0_ffn_kn_w, L0_ffn_gate_w, L0_ffn_e0_up, L0_ffn_e0_down, L0_ffn_e1_w1, L0_ffn_e1_w2, L0_ffn_e1_down, L0_ffn_e2_l1, L0_ffn_e2_l2, L0_ffn_e2_l3, L0_ffn_e2_l4, L0_ffn_e3_down, L0_ffn_e3_up, L0_ffn_e3_out)
    return x

_drawn_inputs = setup_inputs


def setup_inputs(seed=0):
    import zlib

    import numpy as np

    out = dict(_drawn_inputs(seed))
    spreads = {'L0_cond_b_z': (0.0, 0.8),
     'L0_cond_b_r': (0.0, 0.8),
     'L0_cond_b': (0.0, 0.1),
     'L0_cond2_router_bias': (0.0, 0.349),
     'L0_ffn_n1_w': (1.0, 0.6),
     'L0_ffn_n2_w': (1.0, 0.6),
     'L0_ffn_qn_w': (1.0, 0.6),
     'L0_ffn_kn_w': (1.0, 0.6)}
    factors = {'L0_cond_W_z': 8.0,
     'L0_cond_U_z': 8.0,
     'L0_cond_C_z': 8.0,
     'L0_cond_W_r': 8.0,
     'L0_cond_U_r': 29.25,
     'L0_cond_C_r': 8.0,
     'L0_cond_W': 3.889,
     'L0_cond_U': 6.831,
     'L0_cond2_router_W': 4.0,
     'L0_cond2_w1': 4.925,
     'L0_cond2_w3': 4.854,
     'L0_cond2_w2': 4.753,
     'L0_cond2_W1e': 2.761,
     'L0_cond2_W2e': 2.759,
     'L0_ffn_wq': 3.761,
     'L0_ffn_wk': 3.691,
     'L0_ffn_wv': 2.735,
     'L0_ffn_wo': 2.803,
     'L0_ffn_gate_w': 7.624,
     'L0_ffn_e0_up': 3.062,
     'L0_ffn_e0_down': 3.13,
     'L0_ffn_e1_w1': 8.0,
     'L0_ffn_e1_w2': 8.0,
     'L0_ffn_e1_down': 8.0,
     'L0_ffn_e2_l1': 8.0,
     'L0_ffn_e2_l2': 8.0,
     'L0_ffn_e2_l3': 8.0,
     'L0_ffn_e2_l4': 8.0,
     'L0_ffn_e3_down': 8.0,
     'L0_ffn_e3_up': 8.0,
     'L0_ffn_e3_out': 8.0}
    for name, (base, spread) in spreads.items():
        noise = np.random.default_rng([zlib.crc32(name.encode()), seed]).standard_normal(out[name].shape)
        drawn = base * np.exp(spread * noise) if base else spread * noise
        out[name] = jnp.asarray(drawn.astype(out[name].dtype))
    for name, factor in factors.items():
        out[name] = (out[name] * factor).astype(out[name].dtype)
    return out
```

```python
from contextlib import ExitStack

import concourse.bass as bass
from concourse import mybir

F32 = mybir.dt.float32
BF16 = mybir.dt.bfloat16
U32 = mybir.dt.uint32
ALU = mybir.AluOpType
ACT = mybir.ActivationFunctionType
X = mybir.AxisListType.X

P = 128
B, T, D = 4, 256, 128
TC = P // B
NC = T // TC
E1, E2 = 8, 4
HEADS, HD = 16, 8
G = 4
HG = HEADS // G
M_ZERO = 32
EPS = 1.1920929e-07
NEG = -1e30
FLT_MAX = 3.4028234663852886e38

REC = [("W_z", P), ("W_r", P), ("W", P), ("U_z", P), ("U_r", P), ("U", P), ("C_z", P), ("C_r", P), ("C", P)]
VEC = [("b_z", 1), ("b_r", 1), ("b", 1), ("n1", 1), ("n2", 1), ("cond", B), ("rbias", E1), ("qn", HD), ("kn", HD)]
CST = [("ident", P), ("inv", NC * TC), ("head_f", HG), ("head_p", HG), ("pick_t", TC), ("count8", 8),
       ("mask", (2 * NC - 1) * TC)]
MIX = [("rw_x", E1), ("rw_c", E1), ("w1", 2 * P), ("w3", 2 * P), ("w2", 2 * P), ("up", E1 * P), ("down", E1 * P)]
FFN = [("wq", P), ("wk", P), ("wv", P), ("wo", P),
       ("gate", E2), ("e0_up", 2 * P), ("e1_w1", 2 * P), ("e1_w2", 2 * P), ("l1", 2 * P), ("e3_down", P),
       ("e0_down", 2 * P), ("e1_down", 2 * P), ("l2", 4 * P), ("l3", 4 * P), ("l4", 2 * P),
       ("e3_up", 2 * P), ("e3_out", 2 * P)]


def columns(table):
    at, found = 0, {}
    for name, width in table:
        found[name] = (at, at + width)
        at += width
    return found, at


def build(nc, xT, rec, vec, cst, mix, ffn, out):
    with ExitStack() as ctx:
        def sb(name, *shape, dt=F32):
            return ctx.enter_context(nc.sbuf_tensor(name, [P, *shape], dt))

        def bank(name):
            return ctx.enter_context(nc.psum_tensor(name, [P, 512], F32))

        def sem(name):
            return ctx.enter_context(nc.semaphore(name))

        x_sb = sb("x_sb", (NC + 1) * P)
        packs = {}
        for name, table in (("rec", REC), ("vec", VEC), ("cst", CST), ("mix", MIX), ("ffn", FFN)):
            found, width = columns(table)
            packs[name] = (sb(name + "_sb", width), found)

        def part(pack, name, lo=0, n=None):
            t, found = packs[pack]
            a, b = found[name]
            return t[:, a + lo:(b if n is None else a + lo + n)]

        ident = part("cst", "ident")
        u_half = sb("u_half", 3, P)
        gate_bias = sb("gate_bias", 3, B)
        cond_rep = sb("cond_rep", B, TC)
        route_c = sb("route_c", E1)
        qk_scale = sb("qk_scale", P)
        mask_bf = sb("mask_bf", (2 * NC - 1) * TC, dt=BF16)
        ident_bf = sb("ident_bf", P, dt=BF16)
        e_const = sb("e_const", 8)
        neg_half = sb("neg_half", 2 * HEADS)

        h2 = sb("h2", 2, B)
        tz, tr, th = sb("tz", 2, B), sb("tr", 2, B), sb("th", 2, B)
        g_in, keep, kept, new = sb("g_in", 2, B), sb("keep", 2, B), sb("kept", 2, B), sb("new", 2, B)
        run = sb("run", B, TC)

        mean = sb("mean", B, TC)
        x1 = sb("x1", P)
        x1t = sb("x1t", P)
        sm = sb("sm", 64)
        ix1, ix2 = sb("ix1", 8, dt=U32), sb("ix2", 8, dt=U32)
        comb = sb("comb", E1)
        th_sh, s_a, s_h = sb("th_sh", 2, P), sb("s_a", 2, P), sb("s_h", 2, P)
        ge = sb("ge", E1, P)
        acc = sb("acc", P)
        x2 = sb("x2", P)
        sq = sb("sq", 2 * P)
        rs = sb("rs", 8)
        hn, hn_f = sb("hn", P), sb("hn_f", P)
        ss_h, r_h = sb("ss_h", 2 * HEADS), sb("r_h", 2 * HEADS)
        q_n, q_s, k_n = sb("q_n", P), sb("q_s", P), sb("k_n", P)
        q_m = sb("q_m", B, HG, TC)
        k_c = sb("k_c", NC * P)
        v_c = sb("v_c", NC * G * P)
        nmax, psum_r = sb("nmax", 16), sb("psum_r", 16)
        p_e = sb("p_e", 2, NC * P)
        p_t = sb("p_t", 2, NC * P)
        inv_sum = sb("inv_sum", 16)
        ao_m = sb("ao_m", B, G, 32)
        ao_f = sb("ao_f", P)
        xn, xn_f = sb("xn", P), sb("xn_f", P)
        sm2 = sb("sm2", 96)
        wts = sb("wts", 8)
        gf = sb("gf", 11, P)
        th_e, e_a, e_h = sb("th_e", 2, P), sb("e_a", 2, P), sb("e_h", 2, P)
        base = sb("base", P)
        fin = sb("fin", P)

        bk_r, bk_z, bk_h = bank("bk_r"), bank("bk_z"), bank("bk_h")
        b0, b1, b2, b3, b4 = (bank(f"b{i}") for i in range(5))

        in_rec, in_x, in_mix, in_ffn = sem("in_rec"), sem("in_x"), sem("in_mix"), sem("in_ffn")
        u_ready, rec_ps, gb_ready, cr_ready = sem("u_ready"), sem("rec_ps"), sem("gb_ready"), sem("cr_ready")
        rc_ps, dve_setup, pool_setup, filled = sem("rc_ps"), sem("dve_setup"), sem("pool_setup"), sem("filled")
        body_go, out_done = sem("body_go"), sem("out_done")
        begun = {n: sem("begun_" + n) for n in ("pe", "act", "dve", "sp")}

        names = """r_acc z_acc h_acc r_act z_act h_act g_ready keep_ready kept_ready new_ready h_ready run_ready
            mean_ready x1_ready lg_ps nl_ready sig_e dchain comb_ready x1t_ps x1t_ready sh_ps sh_th sa_ready sh_ready
            up_ps ge_ready shd_ps dn_ps acc_ready x2_ready ms_ready r1_ready hn_ready hn_ps hnf_ready qk_ps v_ps
            sq_ready ssh_ready rh_ready qn_ready qs_ready kn_ready qt_ps kt_ps qm_ready kc_ready vc_ready
            sc_ps nmax_ready pe_ready pt_ps pt_ready pv_ps inv_ready aom_ready ao_ps aof_ready wo_ps x3_ready
            ms2_ready r2_ready xn_ready xn_ps xnf_ready gt_ps ge_nl ge_e wts_ready hid_ps hid_ready e1_ps
            e1_th ea_ready eh_ready o_ps moe_ready base_ready body_done""".split()
        S = {n: sem(n) for n in names}
        nums = sorted(s.num for s in S.values())
        assert nums == list(range(nums[0], nums[0] + len(nums)))
        body_sems = range(nums[0], nums[-1] + 1)

        block = ctx.enter_context(nc.Block())

        def pacer(program):
            state = [next(program, None)]

            def advance(step):
                while state[0] is not None and state[0] <= step:
                    state[0] = next(program, None)
            return advance

        def begin(engine, name, n):
            engine.wait_ge(body_go, n)
            engine.sem_inc(begun[name], 1)

        def none():
            return
            yield

        ALL = 1e9
        GP = 3
        END = 21.6 + G * GP + 2

        def bcast(ap, axis, shape):
            return ap.unsqueeze(axis).to_broadcast(shape)

        def tile_cols(tile):
            return bass.ds(tile * P, P)

        @block.tensor
        def _(pe):
            def mm(o, w, r, start=True, stop=True):
                return pe.matmul(o, w, r, start=start, stop=stop, skip_group_check=True)

            def fill(gate, bk, chunk):
                mm(bk[:, 0:P], part("rec", ("W_z", "W_r", "W")[gate]), x_sb[:, tile_cols(chunk)])
                return mm(bk[:, 0:P], ident, bcast(gate_bias[:, gate, :], 2, [P, B, TC]), start=False)

            def at(bk, t):
                return bk[:, t:P:TC]

            def gru(advance, chunk):
                for t in range(TC):
                    if t == 0:
                        mm(at(bk_r, t), u_half[:, 1, :], h2[:, 0, :], start=False).then_inc(S["r_acc"], 1)
                    else:
                        pe.wait_ge(S["kept_ready"], t)
                        mm(at(bk_r, t), u_half[:, 1, :], kept[:, t % 2, :], start=False)
                        advance(t - 0.4)
                        pe.wait_ge(S["new_ready"], t)
                        mm(at(bk_r, t), u_half[:, 1, :], new[:, t % 2, :], start=False).then_inc(S["r_acc"], 1)
                        pe.wait_ge(S["h_ready"], t)
                    mm(at(bk_z, t), u_half[:, 0, :], h2[:, t % 2, :], start=False).then_inc(S["z_acc"], 1)
                    advance(t + 0.1)
                    pe.wait_ge(S["g_ready"], t + 1)
                    mm(at(bk_h, t), u_half[:, 2, :], g_in[:, t % 2, :], start=False).then_inc(S["h_acc"], 1)
                pe.wait_ge(S["z_act"], TC)
                fill(0, bk_z, chunk + 1)
                pe.wait_ge(S["r_act"], TC)
                fill(1, bk_r, chunk + 1)
                pe.wait_ge(S["h_act"], TC)
                fill(2, bk_h, chunk + 1)

            def tile(i, nk):
                keys = nk * TC
                yield 0.6
                pe.wait_ge(S["x1_ready"], 1)
                mm(b0[:, 0:E1], x1[:, :], part("mix", "rw_x")).then_inc(S["lg_ps"], 1)
                yield 1
                pe.transpose(b1[:, 0:P], x1[:, :], ident).then_inc(S["x1t_ps"], 1)
                for j, bk in enumerate((b2, b3)):
                    yield 1.5 + j
                    mm(bk[:, 0:P], part("mix", "w1", j * P, P), x1[:, :])
                    yield 2 + j
                    mm(bk[:, P:2 * P], part("mix", "w3", j * P, P), x1[:, :]).then_inc(S["sh_ps"], 1)
                for e in range(E1):
                    yield 3.6 + e / 2
                    if e == 1:
                        pe.wait_ge(S["x1t_ready"], 1)
                    if e >= 2:
                        pe.wait_ge(S["ge_ready"], e - 1)
                    mm((b4, b1)[e % 2][:, 0:P], part("mix", "up", e * P, P), x1[:, :]).then_inc(S["up_ps"], 1)
                yield 7.6
                pe.wait_ge(S["nl_ready"], 1)
                pe.wait_ge(S["sh_ready"], 2)
                mm(b0[:, 0:P], s_h[:, 0, :], part("mix", "w2", 0, P), stop=False)
                yield 8.1
                mm(b0[:, 0:P], s_h[:, 1, :], part("mix", "w2", P, P), start=False).then_inc(S["shd_ps"], 1)
                for e in range(E1):
                    yield 8.6 + e / 2
                    pe.wait_ge(S["ge_ready"], e + 1)
                    if e >= 2:
                        pe.wait_ge(S["acc_ready"], e - 1)
                    mm((b2, b3)[e % 2][:, 0:P], ge[:, e, :], part("mix", "down", e * P, P)).then_inc(S["dn_ps"], 1)
                yield 14.6
                pe.wait_ge(S["hn_ready"], 1)
                pe.transpose(b4[:, 0:P], hn[:, :], ident).then_inc(S["hn_ps"], 1)
                yield 15.1
                pe.wait_ge(S["hnf_ready"], 1)
                mm(b1[:, 0:P], hn_f[:, :], part("ffn", "wq"))
                mm(b1[:, P:2 * P], hn_f[:, :], part("ffn", "wk")).then_inc(S["qk_ps"], 1)
                yield 15.6
                pe.wait_ge(S["x2_ready"], 1)
                mm(b0[:, 0:P], hn_f[:, :], part("ffn", "wv")).then_inc(S["v_ps"], 1)
                yield 20.1
                pe.wait_ge(S["kn_ready"], 1)
                pe.wait_ge(S["acc_ready"], E1)
                pe.transpose(b2[:, 0:P], k_n[:, :], ident).then_inc(S["kt_ps"], 1)
                pe.wait_ge(S["qs_ready"], 1)
                pe.transpose(b4[:, 0:P], q_s[:, :], ident).then_inc(S["qt_ps"], 1)
                ao = b0[:, :].rearrange("p (b g f) -> p b g f", b=B, g=G)
                for g in range(G + 1):
                    for half in range(2):
                        if g == G:
                            continue
                        u = 2 * g + half
                        bk = (b1, b3)[half]
                        yield 21.6 + g * GP + half / 2
                        if u == 0:
                            pe.wait_ge(S["qm_ready"], HG)
                            pe.wait_ge(S["kc_ready"], 1)
                            pe.wait_ge(S["kn_ready"], 1)
                        if u >= 2:
                            pe.wait_ge(S["pe_ready"], 2 * (u - 1))
                        for m in range(2):
                            b = 2 * half + m
                            o = bk[:, m * keys:(m + 1) * keys]
                            rows = slice(32 * g, 32 * g + 32)
                            mm(o, q_m[rows, b, :, :], k_c[rows, :].rearrange("p (i b t) -> p i b t", b=B, t=TC)[:, 0:nk, b, :],
                               stop=False)
                            last = mm(o, ident_bf[:, :], mask_bf[:, bass.ds((NC - 1 - i) * TC, keys)], start=False)
                        last.then_inc(S["sc_ps"], 1)
                    if g >= 1:
                        h = g - 1
                        yield 22.6 + g * GP
                        pe.wait_ge(S["pe_ready"], 4 * (h + 1))
                        for c0 in range(0, nk, 4):
                            n = c0 // 4
                            if h >= 1:
                                pe.wait_ge(S["pt_ready"], 2 * ((h - 1) * (nk // 4) + n + 1))
                            for c in range(c0, c0 + 4):
                                last = pe.transpose((b4, b2)[n][:, (c % 4) * P:(c % 4 + 1) * P],
                                                    p_e[:, h % 2, c * P:(c + 1) * P], ident)
                            last.then_inc(S["pt_ps"], 1)
                            yield 22.6 + g * GP + (n + 1) / 2
                        yield 23.6 + g * GP
                        if h == 0:
                            pe.wait_ge(S["vc_ready"], B)
                        pe.wait_ge(S["pt_ready"], 2 * (h + 1) * (nk // 4))
                        for c in range(nk):
                            if c % 2 == 0:
                                yield 23.6 + g * GP + c / 8
                            last = mm(ao[:, :, h, :], p_t[:, h % 2, c * P:(c + 1) * P],
                                      v_c[:, (c * G + h) * P:(c * G + h + 1) * P], start=(c == 0), stop=(c == nk - 1))
                        last.then_inc(S["pv_ps"], 1)
                yield END
                pe.wait_ge(S["aom_ready"], HG)
                for b in range(B):
                    last = mm(b1[:, b * TC:(b + 1) * TC], ao_m[:, b, :, :], part("cst", "pick_t"))
                last.then_inc(S["ao_ps"], 1)
                yield END + 0.5
                pe.wait_ge(S["aof_ready"], 1)
                mm(b3[:, 0:P], ao_f[:, :], part("ffn", "wo")).then_inc(S["wo_ps"], 1)
                yield END + 2
                pe.wait_ge(S["xn_ready"], 1)
                pe.transpose(b1[:, 0:P], xn[:, :], ident).then_inc(S["xn_ps"], 1)
                yield END + 2.5
                pe.wait_ge(S["xnf_ready"], 1)
                mm(b0[:, 0:E2], xn_f[:, :], part("ffn", "gate")).then_inc(S["gt_ps"], 1)

                def hidden(n, pieces):
                    if n == 0:
                        pe.wait_ge(S["pt_ready"], 2 * G * (nk // 4))
                    if n >= 2:
                        pe.wait_ge(S["hid_ready"], n - 1)
                    for k, (w, r) in enumerate(pieces):
                        last = mm((b4, b2)[n % 2][:, 0:P], w, r, start=(k == 0), stop=(k == len(pieces) - 1))
                    last.then_inc(S["hid_ps"], 1)

                f = lambda name, k=0: part("ffn", name, k * P, P)
                for k in range(2):
                    yield END + 2.6 + k / 5
                    hidden(k, [(f("e0_up", k), xn_f[:, :])])
                for k in range(2):
                    yield END + 3 + k / 5
                    hidden(2 + k, [(f("l1", k), xn_f[:, :])])
                for j, bk in enumerate((b1, b3)):
                    yield END + 3.2 + j / 5
                    mm(bk[:, 0:P], f("e1_w1", j), xn_f[:, :])
                    mm(bk[:, P:2 * P], f("e1_w2", j), xn_f[:, :]).then_inc(S["e1_ps"], 1)
                yield END + 3.5
                hidden(4, [(f("e3_down"), xn_f[:, :])])
                for k in range(2):
                    yield END + 3.6 + k / 5
                    pe.wait_ge(S["hid_ready"], 4)
                    hidden(5 + k, [(f("l2", 2 * k), gf[:, 2, :]), (f("l2", 2 * k + 1), gf[:, 3, :])])
                for k in range(2):
                    yield END + 4 + k / 5
                    pe.wait_ge(S["hid_ready"], 5)
                    hidden(7 + k, [(f("e3_up", k), gf[:, 4, :])])
                yield END + 4.2
                pe.wait_ge(S["ge_nl"], 1)
                mm(b0[:, 0:P], gf[:, 0, :], f("e0_down", 0), stop=False)
                mm(b0[:, 0:P], gf[:, 1, :], f("e0_down", 1), start=False).then_inc(S["o_ps"], 1)
                for k in range(2):
                    yield END + 4.4 + k / 5
                    pe.wait_ge(S["hid_ready"], 7)
                    hidden(9 + k, [(f("l3", 2 * k), gf[:, 5, :]), (f("l3", 2 * k + 1), gf[:, 6, :])])
                yield END + 4.6
                pe.wait_ge(S["eh_ready"], 2)
                mm(b1[:, 0:P], e_h[:, 0, :], f("e1_down", 0), stop=False)
                mm(b1[:, 0:P], e_h[:, 1, :], f("e1_down", 1), start=False).then_inc(S["o_ps"], 1)
                yield END + 4.8
                pe.wait_ge(S["hid_ready"], 9)
                mm(b3[:, 0:P], gf[:, 7, :], f("e3_out", 0), stop=False)
                mm(b3[:, 0:P], gf[:, 8, :], f("e3_out", 1), start=False).then_inc(S["o_ps"], 1)
                yield END + 5
                pe.wait_ge(S["hid_ready"], 11)
                pe.wait_ge(S["moe_ready"], 1)
                mm(b0[:, 0:P], gf[:, 9, :], f("l4", 0), stop=False)
                mm(b0[:, 0:P], gf[:, 10, :], f("l4", 1), start=False).then_inc(S["o_ps"], 1)

            pe.wait_ge(in_rec, 3 * 16)
            for gate in range(3):
                last = mm(b0[:, gate * B:(gate + 1) * B], part("rec", ("C_z", "C_r", "C")[gate]), part("vec", "cond"))
            last.then_inc(rec_ps, 1)
            pe.wait_ge(in_x, 16)
            pe.wait_ge(gb_ready, 3)
            fill(0, bk_z, 0)
            fill(1, bk_r, 0)
            fill(2, bk_h, 0)
            pe.wait_ge(u_ready, 4)
            gru(pacer(none()), 0)
            pe.wait_ge(in_mix, 16)
            pe.wait_ge(cr_ready, 1)
            mm(b1[:, 0:E1], cond_rep[:, :, :], part("mix", "rw_c")).then_inc(rc_ps, 1)
            pe.drain().then_inc(S["body_done"], 1)
            with pe.Fori(1, NC // 2 + 1) as c:
                begin(pe, "pe", c)
                advance = pacer(tile(c - 1, NC // 2))
                gru(advance, c)
                advance(ALL)
                pe.drain().then_inc(S["body_done"], 1)
            with pe.Fori(NC // 2 + 1, NC) as c:
                begin(pe, "pe", c)
                advance = pacer(tile(c - 1, NC))
                gru(advance, c)
                advance(ALL)
                pe.drain().then_inc(S["body_done"], 1)
            begin(pe, "pe", NC)
            pacer(tile(NC - 1, NC))(ALL)

        @block.scalar
        def _(act):
            def at(bk, t):
                return bk[:, t:P:TC]

            def gru(advance):
                for t in range(TC):
                    act.wait_ge(S["r_acc"], t + 1)
                    act.activation(tr[:, t % 2, :], at(bk_r, t), ACT.Tanh, scale=0.5).then_inc(S["r_act"], 1)
                    act.wait_ge(S["z_acc"], t + 1)
                    act.activation(tz[:, t % 2, :], at(bk_z, t), ACT.Tanh, scale=0.5).then_inc(S["z_act"], 1)
                    advance(t + 0.3)
                    act.wait_ge(S["h_acc"], t + 1)
                    act.activation(th[:, t % 2, :], at(bk_h, t), ACT.Tanh).then_inc(S["h_act"], 1)
                    advance(t + 0.7)

            def tile(i, nk):
                keys = nk * TC
                yield 1.2
                act.wait_ge(S["x1t_ps"], 1)
                act.copy(x1t[:, :], b1[:, 0:P]).then_inc(S["x1t_ready"], 1)
                for j, bk in enumerate((b2, b3)):
                    yield 2.2 + j
                    act.wait_ge(S["sh_ps"], j + 1)
                    act.activation(th_sh[:, j, :], bk[:, 0:P], ACT.Tanh, scale=0.5).then_inc(S["sh_th"], 1)
                for e in range(E1):
                    yield 3.7 + e / 2
                    act.wait_ge(S["up_ps"], e + 1)
                    act.activation(ge[:, e, :], (b4, b1)[e % 2][:, 0:P], ACT.Gelu).then_inc(S["ge_ready"], 1)
                yield 14.7
                act.wait_ge(S["hn_ps"], 1)
                act.copy(hn_f[:, :], b4[:, 0:P]).then_inc(S["hnf_ready"], 1)
                yield 15.3
                act.wait_ge(S["qk_ps"], 1)
                act.activation(sq[:, :], b1[:, 0:2 * P], ACT.Square).then_inc(S["sq_ready"], 1)
                for b in range(B):
                    yield 16.3 + b / 4
                    rows = slice(TC * b, TC * (b + 1))
                    act.wait_ge(S["v_ps"], 1)
                    act.copy(v_c[rows, bass.ds(i * (G * P), G * P)].rearrange("p (g b f) -> p g b f", g=G, b=B)[:, :, b, :],
                             b0[rows, 0:P].rearrange("p (g f) -> p g f", g=G)).then_inc(S["vc_ready"], 1)
                yield 20.3
                act.wait_ge(S["kt_ps"], 1)
                act.copy(k_c[:, tile_cols(i)], b2[:, 0:P]).then_inc(S["kc_ready"], 1)
                for h in range(HG):
                    yield 20.3 + h / 4
                    act.wait_ge(S["qt_ps"], 1)
                    act.activation(q_m[:, :, h, :], b4[:, 0:P].rearrange("p (b t) -> p b t", b=B), ACT.Identity,
                                   scale=part("cst", "head_f", h, 1)).then_inc(S["qm_ready"], 1)
                for g in range(G + 1):
                    for half in range(2):
                        if g == G:
                            continue
                        u = 2 * g + half
                        yield 22.3 + g * GP + half / 2
                        act.wait_ge(S["nmax_ready"], u + 1)
                        if u % 2 == 0 and g >= 2:
                            act.wait_ge(S["pt_ps"], (g - 1) * (nk // 4))
                        for m in range(2):
                            b = 2 * half + m
                            o = p_e[:, g % 2, :].rearrange("p (c b t) -> p c b t", b=B, t=TC)[:, 0:nk, b, :]
                            s = (b1, b3)[half][:, m * keys:(m + 1) * keys].rearrange("p (c t) -> p c t", t=TC)
                            act.activation(o, s, ACT.Exp, bias=nmax[:, 2 * u + m:2 * u + m + 1],
                                           accum_out=psum_r[:, b * G + g:b * G + g + 1]).then_inc(S["pe_ready"], 1)
                    if g >= 1:
                        h = g - 1
                        for n in range(nk // 4):
                            yield 22.8 + g * GP + n / 2
                            act.wait_ge(S["pt_ps"], h * (nk // 4) + n + 1)
                            if h >= 2 and n == 0:
                                act.wait_ge(S["pv_ps"], h - 1)
                            for m in range(2):
                                lo = n * 512 + m * 256
                                act.copy(p_t[:, h % 2, lo:lo + 256],
                                         (b4, b2)[n][:, m * 256:m * 256 + 256]).then_inc(S["pt_ready"], 1)
                                yield 22.8 + g * GP + n / 2 + (m + 1) / 2.5
                yield END + 0.3
                act.wait_ge(S["ao_ps"], 1)
                act.copy(ao_f[:, :], b1[:, 0:P]).then_inc(S["aof_ready"], 1)
                yield END + 2.2
                act.wait_ge(S["xn_ps"], 1)
                act.copy(xn_f[:, :], b1[:, 0:P]).then_inc(S["xnf_ready"], 1)

                def gelu(n):
                    act.wait_ge(S["hid_ps"], n + 1)
                    act.activation(gf[:, n, :], (b4, b2)[n % 2][:, 0:P], ACT.Gelu).then_inc(S["hid_ready"], 1)

                for n in range(4):
                    yield END + 2.8 + n / 5
                    gelu(n)
                for j, bk in enumerate((b1, b3)):
                    yield END + 3.4 + j / 5
                    act.wait_ge(S["e1_ps"], j + 1)
                    act.activation(th_e[:, j, :], bk[:, 0:P], ACT.Tanh, scale=0.5).then_inc(S["e1_th"], 1)
                for n in range(4, 11):
                    yield END + 3.6 + n / 5
                    gelu(n)

            act.preload_act_table(ACT.Gelu)
            gru(pacer(none()))
            act.drain().then_inc(S["body_done"], 1)
            with act.Fori(1, NC // 2 + 1) as c:
                begin(act, "act", c)
                advance = pacer(tile(c - 1, NC // 2))
                gru(advance)
                advance(ALL)
                act.drain().then_inc(S["body_done"], 1)
            with act.Fori(NC // 2 + 1, NC) as c:
                begin(act, "act", c)
                advance = pacer(tile(c - 1, NC))
                gru(advance)
                advance(ALL)
                act.drain().then_inc(S["body_done"], 1)
            begin(act, "act", NC)
            pacer(tile(NC - 1, NC))(ALL)

        @block.vector
        def _(dve):
            def gru(advance):
                def add_run(t):
                    dve.wait_ge(S["h_ready"], t + 1)
                    if t >= 1:
                        dve.wait_ge(S["run_ready"], t)
                    prev = (t - 1) % TC
                    dve.tensor_tensor(run[:, :, t], run[:, :, prev], h2[:, (t + 1) % 2, :],
                                      ALU.add).then_inc(S["run_ready"], 1)

                for t in range(TC):
                    h, nxt = h2[:, t % 2, :], (t + 1) % 2
                    dve.wait_ge(S["r_act"], t + 1)
                    if t >= 1:
                        dve.wait_ge(S["h_ready"], t)
                    dve.scalar_tensor_tensor(g_in[:, t % 2, :], tr[:, t % 2, :], 1.0, h, ALU.add,
                                             ALU.mult).then_inc(S["g_ready"], 1)
                    if t >= 1:
                        add_run(t - 1)
                    advance(t + 0.2)
                    dve.wait_ge(S["z_act"], t + 1)
                    dve.tensor_scalar(keep[:, t % 2, :], tz[:, t % 2, :], -0.5, 0.5, ALU.mult,
                                      ALU.add).then_inc(S["keep_ready"], 1)
                    dve.wait_ge(S["keep_ready"], t + 1)
                    dve.tensor_tensor(kept[:, nxt, :], keep[:, t % 2, :], h, ALU.mult).then_inc(S["kept_ready"], 1)
                    advance(t + 0.4)
                    dve.wait_ge(S["h_act"], t + 1)
                    dve.scalar_tensor_tensor(new[:, nxt, :], tz[:, t % 2, :], 1.0, th[:, t % 2, :], ALU.add,
                                             ALU.mult).then_inc(S["new_ready"], 1)
                    dve.wait_ge(S["new_ready"], t + 1)
                    dve.tensor_tensor(h2[:, nxt, :], kept[:, nxt, :], new[:, nxt, :],
                                      ALU.add).then_inc(S["h_ready"], 1)
                    advance(t + 0.8)
                add_run(TC - 1)

            chain = [0]

            def step(ins):
                chain[0] += 1
                ins.then_inc(S["dchain"], 1)

            def after():
                dve.wait_ge(S["dchain"], chain[0])

            def two_best(v, mx, ix, ixf, first, mask, w):
                after()
                step(dve.max(mx, v))
                yield w + 0.2
                after()
                step(dve.max_index(ix, mx, v))
                yield w + 0.8
                after()
                step(dve.tensor_copy(ixf, ix))
                yield w + 1.2
                after()
                step(dve.tensor_scalar(first, part("cst", "count8"), ixf[:, 0:1], None, ALU.is_equal))
                yield w + 1.8
                after()
                step(dve.scalar_tensor_tensor(mask, part("cst", "count8"), ixf[:, 1:2], first, ALU.is_equal, ALU.add))

            def swiglu(sems, banks, t_h, a_, h_, w, gap):
                ps, thr, ar, hr = sems
                for j, bk in enumerate(banks):
                    yield w + j * gap
                    dve.wait_ge(S[thr], j + 1)
                    dve.scalar_tensor_tensor(a_[:, j, :], t_h[:, j, :], 1.0, bk[:, 0:P], ALU.add,
                                             ALU.mult).then_inc(S[ar], 1)
                    yield w + j * gap + gap / 2
                    dve.wait_ge(S[ar], j + 1)
                    dve.tensor_tensor(h_[:, j, :], a_[:, j, :], bk[:, P:2 * P], ALU.mult).then_inc(S[hr], 1)

            def tile(i, nk):
                chain[0] = 0
                keys = nk * TC
                inv = part("cst", "inv").rearrange("p (c t) -> p c t", t=TC)
                dve.tensor_tensor(mean[:, :, :], run[:, :, :],
                                  inv[:, bass.ds(i, 1), :].to_broadcast([P, B, TC]), ALU.mult).then_inc(S["mean_ready"], 1)
                dve.wait_ge(S["mean_ready"], 1)
                dve.tensor_tensor(x1[:, :], mean[:, :, :].rearrange("p b t -> p (b t)"), x_sb[:, tile_cols(i)],
                                  ALU.add).then_inc(S["x1_ready"], 1)
                nl, e1, s, sel = (sm[:, 8 * k:8 * k + 8] for k in range(4))
                mx, ixf, first, mask = (sm[:, 8 * k:8 * k + 8] for k in range(4, 8))
                yield 1.4
                dve.wait_ge(S["lg_ps"], 1)
                dve.scalar_tensor_tensor(nl, b0[:, 0:E1], -1.0, route_c[:, :], ALU.mult,
                                         ALU.subtract).then_inc(S["nl_ready"], 1)
                yield 2.2
                dve.wait_ge(S["sig_e"], 1)
                step(dve.tensor_scalar(e1, e1, 1.0, None, ALU.add))
                yield 2.4
                after()
                step(dve.reciprocal(s, e1))
                yield from swiglu(("sh_ps", "sh_th", "sa_ready", "sh_ready"), (b2, b3), th_sh, s_a, s_h, 2.6, 1)
                yield 4.2
                after()
                step(dve.tensor_tensor(sel, s, part("vec", "rbias"), ALU.add))
                yield 4.4
                yield from two_best(sel, mx, ix1[:, :], ixf, first, mask, 4.6)
                yield 6.6
                after()
                den, ok = mx[:, 0:1], mx[:, 1:2]
                step(dve.scalar_tensor_tensor(sel, mask, 1.0, s, ALU.mult, ALU.mult, accum_out=den))
                yield 6.8
                after()
                step(dve.tensor_scalar(ok, den, 1e-9, None, ALU.is_gt))
                yield 7.2
                step(dve.tensor_scalar(mx[:, 2:3], den, 1e-9, None, ALU.add))
                yield 7.2
                after()
                step(dve.reciprocal(mx[:, 3:4], mx[:, 2:3]))
                yield 7.4
                step(dve.tensor_scalar(mx[:, 4:5], ok, -0.5, 0.5, ALU.mult, ALU.add))
                yield 7.8
                after()
                step(dve.tensor_tensor(mx[:, 5:6], mx[:, 3:4], ok, ALU.mult))
                yield 8.2
                after()
                step(dve.tensor_scalar(first, mask, mx[:, 4:5], None, ALU.mult))
                yield 8.4
                after()
                dve.scalar_tensor_tensor(comb[:, :], sel, mx[:, 5:6], first, ALU.mult,
                                         ALU.add).then_inc(S["comb_ready"], 1)
                for e in range(E1):
                    yield 8.8 + e / 2
                    dve.wait_ge(S["dn_ps"], e + 1)
                    y, w = (b2, b3)[e % 2][:, 0:P], comb[:, e:e + 1]
                    if e == 0:
                        dve.wait_ge(S["comb_ready"], 1)
                        dve.tensor_scalar(acc[:, :], y, w, None, ALU.mult).then_inc(S["acc_ready"], 1)
                    else:
                        dve.wait_ge(S["acc_ready"], e)
                        dve.scalar_tensor_tensor(acc[:, :], y, w, acc[:, :], ALU.mult, ALU.add).then_inc(S["acc_ready"], 1)
                yield 12.8
                dve.wait_ge(S["shd_ps"], 1)
                dve.wait_ge(S["acc_ready"], E1)
                step(dve.scalar_tensor_tensor(x2[:, :], b0[:, 0:P], 0.5, acc[:, :], ALU.mult, ALU.add))
                yield 13.2
                after()
                dve.tensor_scalar(x2[:, :], x2[:, :], 1.0 / 3.0, None, ALU.mult).then_inc(S["x2_ready"], 1)
                yield 13.4
                dve.wait_ge(S["x2_ready"], 1)
                step(dve.scalar_tensor_tensor(acc[:, :], x2[:, :], 1.0, x2[:, :], ALU.mult, ALU.mult,
                                              accum_out=rs[:, 0:1]))
                yield 13.8
                after()
                dve.tensor_scalar(rs[:, 1:2], rs[:, 0:1], 1.0 / D, EPS, ALU.mult, ALU.add).then_inc(S["ms_ready"], 1)
                yield 14.4
                dve.wait_ge(S["r1_ready"], 1)
                dve.tensor_scalar(hn[:, :], x2[:, :], rs[:, 2:3], None, ALU.mult).then_inc(S["hn_ready"], 1)
                yield 15.8
                dve.wait_ge(S["sq_ready"], 1)
                step(dve.tensor_reduce(ss_h[:, :], sq[:, :].rearrange("p (h d) -> p h d", d=HD), X, ALU.add))
                yield 16.2
                after()
                dve.tensor_scalar(ss_h[:, :], ss_h[:, :], 1.0 / HD, EPS, ALU.mult, ALU.add).then_inc(S["ssh_ready"], 1)
                yield 19.4
                dve.wait_ge(S["rh_ready"], 1)
                heads = lambda ap: ap.rearrange("p (h d) -> p h d", d=HD)
                dve.tensor_tensor(heads(q_n[:, :]), heads(b1[:, 0:P]), bcast(r_h[:, 0:HEADS], 2, [P, HEADS, HD]),
                                  ALU.mult).then_inc(S["qn_ready"], 1)
                yield 19.8
                dve.tensor_tensor(heads(k_n[:, :]), heads(b1[:, P:2 * P]), bcast(r_h[:, HEADS:], 2, [P, HEADS, HD]),
                                  ALU.mult).then_inc(S["kn_ready"], 1)
                yield 19.8
                dve.wait_ge(S["qn_ready"], 1)
                dve.tensor_tensor(q_s[:, :], q_n[:, :], qk_scale[:, :], ALU.mult).then_inc(S["qs_ready"], 1)
                for u in range(2 * G):
                    yield 21.8 + (u // 2) * GP + u % 2 / 2
                    dve.wait_ge(S["sc_ps"], u + 1)
                    dve.tensor_reduce(nmax[:, 2 * u:2 * u + 2], (b1, b3)[u % 2][:, 0:2 * keys].rearrange("p (m k) -> p m k", m=2),
                                      X, ALU.max, negate=True).then_inc(S["nmax_ready"], 1)
                yield END - 0.5
                dve.wait_ge(S["pe_ready"], 4 * G)
                dve.reciprocal(inv_sum[:, :], psum_r[:, :]).then_inc(S["inv_ready"], 1)
                dve.wait_ge(S["inv_ready"], 1)
                for h in range(HG):
                    yield END - 0.2
                    dve.wait_ge(S["pv_ps"], G)
                    o = ao_m[:, :, :, h * HD:(h + 1) * HD].rearrange("p b g d -> p (b g) d")
                    s_ = b0[:, :].rearrange("p (n f) -> p n f", f=32)[:, :, h * HD:(h + 1) * HD]
                    dve.scalar_tensor_tensor(o, s_, part("cst", "head_p", h, 1), bcast(inv_sum[:, :], 2, [P, 16, HD]),
                                             ALU.mult, ALU.mult).then_inc(S["aom_ready"], 1)
                yield END + 0.8
                dve.wait_ge(S["wo_ps"], 1)
                dve.tensor_tensor(x2[:, M_ZERO:], x2[:, M_ZERO:], b3[:, M_ZERO:P], ALU.add).then_inc(S["x3_ready"], 1)
                dve.wait_ge(S["x3_ready"], 1)
                step(dve.scalar_tensor_tensor(acc[:, :], x2[:, :], 1.0, x2[:, :], ALU.mult, ALU.mult,
                                              accum_out=rs[:, 3:4]))
                yield END + 1
                after()
                dve.tensor_scalar(rs[:, 4:5], rs[:, 3:4], 1.0 / D, EPS, ALU.mult, ALU.add).then_inc(S["ms2_ready"], 1)
                yield END + 1.2
                dve.wait_ge(S["x1t_ready"], 1)
                dve.tensor_tensor(base[:, :], x2[:, :], x1t[:, :], ALU.add).then_inc(S["base_ready"], 1)
                yield END + 1.4
                dve.wait_ge(S["r2_ready"], 1)
                dve.tensor_scalar(xn[:, :], x2[:, :], rs[:, 5:6], None, ALU.mult).then_inc(S["xn_ready"], 1)
                lg, eq, clean, ex, pr, mx2, ixf2, first2, mask2, pk = (sm2[:, 8 * k:8 * k + 8] for k in range(10))
                cols = slice(0, E2)
                yield END + 2.7
                step(dve.memset(clean[:, cols], 0.0))
                dve.memset(pr, -1.0)
                dve.wait_ge(S["gt_ps"], 1)
                dve.tensor_copy(lg[:, cols], b0[:, 0:E2]).then_inc(S["ge_nl"], 1)
                dve.wait_ge(S["ge_nl"], 1)
                step(dve.tensor_tensor(eq.bitcast(U32)[:, cols], lg[:, cols], lg[:, cols], ALU.is_equal))
                after()
                step(dve.copy_predicated(clean[:, cols], eq.bitcast(U32)[:, cols], lg[:, cols]))
                yield END + 2.9
                after()
                step(dve.tensor_scalar(clean[:, cols], clean[:, cols], FLT_MAX, -FLT_MAX, ALU.min, ALU.max))
                after()
                step(dve.tensor_reduce(rs[:, 6:7], clean[:, cols], X, ALU.max))
                yield END + 3.1
                after()
                dve.tensor_scalar(ex[:, cols], clean[:, cols], rs[:, 6:7], None, ALU.subtract).then_inc(S["ge_e"], 1)
                yield END + 3.8
                dve.wait_ge(S["wts_ready"], 1)
                step(dve.tensor_reduce(rs[:, 6:7], lg[:, cols], X, ALU.add))
                after()
                step(dve.reciprocal(rs[:, 7:8], rs[:, 6:7]))
                after()
                step(dve.tensor_scalar(pr[:, cols], lg[:, cols], rs[:, 7:8], None, ALU.mult))
                yield from swiglu(("e1_ps", "e1_th", "ea_ready", "eh_ready"), (b1, b3), th_e, e_a, e_h, END + 4, 0.2)
                yield from two_best(pr, mx2, ix2[:, :], ixf2, first2, mask2, END + 4.2)
                after()
                step(dve.scalar_tensor_tensor(pk, mask2, 1.0, pr, ALU.mult, ALU.mult, accum_out=mx2[:, 0:1]))
                after()
                step(dve.tensor_scalar(mx2[:, 1:2], mx2[:, 0:1], 1e-8, None, ALU.add))
                after()
                step(dve.reciprocal(mx2[:, 2:3], mx2[:, 1:2]))
                after()
                step(dve.tensor_scalar(wts[:, :], pk, mx2[:, 2:3], None, ALU.mult))
                after()
                step(dve.tensor_scalar(mx2[:, 3:4], wts[:, 1:2], 0.5, None, ALU.mult))
                after()
                w_of = (wts[:, 0:1], mx2[:, 3:4], wts[:, 3:4], wts[:, 2:3])
                dve.wait_ge(S["base_ready"], 1)
                step(dve.tensor_copy(fin[:, :], base[:, :]))
                after()
                for k, bk in enumerate((b0, b1, b3, b0)):
                    yield END + 5.2 + k / 8
                    dve.wait_ge(S["o_ps"], k + 1)
                    if k:
                        dve.wait_ge(S["moe_ready"], k)
                    dve.scalar_tensor_tensor(fin[:, M_ZERO:], bk[:, M_ZERO:P], w_of[k], fin[:, M_ZERO:], ALU.mult,
                                             ALU.add).then_inc(S["moe_ready"], 1)

            dve.memset(h2[:, :, :], 0.0).then_inc(dve_setup, 1)
            dve.memset(run[:, :, :], 0.0).then_inc(dve_setup, 1)
            dve.memset(x_sb[:, NC * P:], 0.0).then_inc(dve_setup, 1)
            dve.wait_ge(in_rec, 3 * 16)
            dve.wait_ge(rec_ps, 1)
            for gate in range(3):
                dve.tensor_scalar(gate_bias[:, gate, :], b0[:, gate * B:(gate + 1) * B],
                                  part("vec", ("b_z", "b_r", "b")[gate]), None, ALU.add).then_inc(gb_ready, 1)
            for gate, (name, f) in enumerate((("U_z", 0.5), ("U_r", 0.5), ("U", 0.25))):
                dve.tensor_scalar(u_half[:, gate, :], part("rec", name), f, None, ALU.mult).then_inc(u_ready, 1)
            dve.wait_ge(dve_setup, 3)
            dve.tensor_copy(cond_rep[:, :, :], bcast(part("vec", "cond"), 2, [P, B, TC])).then_inc(cr_ready, 1)
            dve.wait_ge(cr_ready, 1)
            dve.tensor_copy(mask_bf[:, :], part("cst", "mask")).then_inc(u_ready, 1)
            dve.tensor_copy(ident_bf[:, :], ident).then_inc(dve_setup, 1)
            dve.tensor_tensor(sm[:, 0:HD], part("vec", "qn"), part("vec", "kn"), ALU.mult).then_inc(dve_setup, 1)
            dve.wait_ge(dve_setup, 5)
            dve.tensor_scalar(sm[:, 8:16], sm[:, 0:HD], HD ** -0.5, None, ALU.mult).then_inc(dve_setup, 1)
            dve.wait_ge(dve_setup, 6)
            dve.tensor_copy(qk_scale[:, :].rearrange("p (h d) -> p h d", d=HD), bcast(sm[:, 8:16], 1, [P, HEADS, HD])).then_inc(dve_setup, 1)
            gru(pacer(none()))
            dve.wait_ge(in_ffn, 16)
            for lo, hi, w in (("wq", "wv", "n1"), ("gate", "e3_down", "n2")):
                t, found = packs["ffn"]
                cols = t[:, found[lo][0]:found[hi][1]]
                dve.tensor_scalar(cols, cols, part("vec", w), None, ALU.mult).then_inc(dve_setup, 1)
            dve.wait_ge(rc_ps, 1)
            dve.tensor_copy(route_c[:, :], b1[:, 0:E1]).then_inc(dve_setup, 1)
            dve.drain().then_inc(S["body_done"], 1)
            with dve.Fori(1, NC // 2 + 1) as c:
                begin(dve, "dve", c)
                advance = pacer(tile(c - 1, NC // 2))
                gru(advance)
                advance(ALL)
                dve.drain().then_inc(S["body_done"], 1)
            with dve.Fori(NC // 2 + 1, NC) as c:
                begin(dve, "dve", c)
                advance = pacer(tile(c - 1, NC))
                gru(advance)
                advance(ALL)
                dve.drain().then_inc(S["body_done"], 1)
            begin(dve, "dve", NC)
            pacer(tile(NC - 1, NC))(ALL)

        @block.gpsimd
        def _(pool):
            def tile():
                pool.wait_ge(S["nl_ready"], 1)
                pool.tensor_tensor(sm[:, 8:16], e_const[:, :], sm[:, 0:8], ALU.pow).then_inc(S["sig_e"], 1)
                pool.wait_ge(S["ms_ready"], 1)
                pool.tensor_tensor(rs[:, 2:3], rs[:, 1:2], neg_half[:, 0:1], ALU.pow).then_inc(S["r1_ready"], 1)
                pool.wait_ge(S["ssh_ready"], 1)
                pool.tensor_tensor(r_h[:, :], ss_h[:, :], neg_half[:, :], ALU.pow).then_inc(S["rh_ready"], 1)
                pool.wait_ge(S["ms2_ready"], 1)
                pool.tensor_tensor(rs[:, 5:6], rs[:, 4:5], neg_half[:, 0:1], ALU.pow).then_inc(S["r2_ready"], 1)
                pool.wait_ge(S["ge_e"], 1)
                pool.tensor_tensor(sm2[:, 0:E2], e_const[:, 0:E2], sm2[:, 24:24 + E2], ALU.pow).then_inc(S["wts_ready"], 1)

            def next_pass():
                pool.wait_ge(S["body_done"], 4)
                pool.sem_clear(body_sems)
                pool.drain().then_inc(body_go, 1)

            pool.memset(e_const[:, :], 2.718281828459045)
            pool.memset(neg_half[:, :], -0.5)
            pool.memset(v_c[:, :], 0.0)
            pool.memset(k_c[:, :], 0.0).then_inc(pool_setup, 1)
            pool.wait_ge(pool_setup, 1)
            next_pass()
            with pool.Fori(1, NC):
                tile()
                next_pass()
            tile()

        @block.sync
        def _(sp):
            sp.dma_start(packs["rec"][0][:, :], rec[:, :]).then_inc(in_rec, 16)
            sp.dma_start(packs["vec"][0][:, :], vec[:, :]).then_inc(in_rec, 16)
            sp.dma_start(packs["cst"][0][:, :], cst[:, :]).then_inc(in_rec, 16)
            sp.dma_start(x_sb[:, 0:NC * P], xT[:, :]).then_inc(in_x, 16)
            sp.dma_start(packs["mix"][0][:, :], mix[:, :]).then_inc(in_mix, 16)
            sp.dma_start(packs["ffn"][0][:, :], ffn[:, :]).then_inc(in_ffn, 16)
            sp.wait_ge(in_mix, 16)
            sp.wait_ge(in_ffn, 16)
            sp.sem_inc(S["body_done"], 1)
            with sp.Fori(1, NC) as c:
                begin(sp, "sp", c)
                sp.wait_ge(S["moe_ready"], E2)
                sp.dma_start(out[bass.ds(c - 1, 1), :, :].rearrange("a p f -> (a p) f"), fin[:, :]).then_inc(out_done, 16)
                sp.wait_ge(out_done, 16 * c)
                sp.sem_inc(S["body_done"], 1)
            begin(sp, "sp", NC)
            sp.wait_ge(S["moe_ready"], E2)
            sp.dma_start(out[NC - 1, :, :], fin[:, :]).then_inc(out_done, 16)
            sp.wait_ge(out_done, 16 * NC)


def constants():
    import numpy as np
    p = np.arange(P)[:, None]
    t = np.arange(TC)[None, :]
    inv = np.broadcast_to(0.5 / (np.arange(T) + 1.0), (P, T))
    mask = np.where(np.arange((2 * NC - 1) * TC)[None, :] - (NC - 1) * TC <= p % TC, 0.0, NEG)
    made = {"ident": np.eye(P), "inv": inv, "head_f": p // HD % HG == np.arange(HG)[None, :],
            "head_p": p // TC == np.arange(HG)[None, :], "pick_t": p % TC == t,
            "count8": np.broadcast_to(np.arange(8), (P, 8)), "mask": mask}
    return np.concatenate([np.asarray(made[n], np.float32).reshape(P, w) for n, w in CST], axis=1)


def kernel(**inputs):
    import numpy as np
    import concourse.bacc as bacc
    from concourse import mybir as mb
    from concourse.bass_utils import run_bass_kernel_spmd as run_spmd

    a = {n: np.asarray(v) for n, v in inputs.items()}

    def rows(w):
        return np.concatenate(np.split(w, w.shape[0] // P, axis=0), axis=1)

    def square(w):
        return np.concatenate([w[k * P:(k + 1) * P, j * P:(j + 1) * P] for j in range(2) for k in range(2)], axis=1)

    col = lambda v: v.reshape(P, 1)
    wide = lambda v: np.broadcast_to(v, (P, v.shape[0]))
    c, m, f = "L0_cond_", "L0_cond2_", "L0_ffn_"
    rec = [a[c + n] for n, _ in REC]
    vec = [col(a[c + "b_z"]), col(a[c + "b_r"]), col(a[c + "b"]), col(a[f + "n1_w"]), col(a[f + "n2_w"]),
           a["cond_1024"].T, wide(a[m + "router_bias"]), wide(a[f + "qn_w"]), wide(a[f + "kn_w"])]
    mix = [a[m + "router_W"][:P], a[m + "router_W"][P:], a[m + "w1"], a[m + "w3"], rows(a[m + "w2"]),
           *a[m + "W1e"], *a[m + "W2e"]]
    ffn = [a[f + "wq"].T, a[f + "wk"].T, a[f + "wv"].T, a[f + "wo"].T,
           a[f + "gate_w"].T, a[f + "e0_up"].T, a[f + "e1_w1"].T, a[f + "e1_w2"].T, a[f + "e2_l1"].T, a[f + "e3_down"].T,
           rows(a[f + "e0_down"].T), rows(a[f + "e1_down"].T), square(a[f + "e2_l2"].T), square(a[f + "e2_l3"].T),
           rows(a[f + "e2_l4"].T), a[f + "e3_up"].T, rows(a[f + "e3_out"].T)]
    x = a["x"].reshape(B, NC, TC, D).transpose(3, 1, 0, 2).reshape(D, NC * P)
    arrays = {"xT": x, "rec": np.concatenate(rec, 1), "vec": np.concatenate(vec, 1), "cst": constants(),
              "mix": np.concatenate(mix, 1), "ffn": np.concatenate(ffn, 1)}
    arrays = {n: np.ascontiguousarray(v) for n, v in arrays.items()}

    nc = bacc.Bacc("TRN2", target_bir_lowering=False, num_devices=1)
    aps = [nc.dram_tensor(n, v.shape, mb.dt.float32, kind="ExternalInput").ap() for n, v in arrays.items()]
    out = nc.dram_tensor("out", (NC, P, D), mb.dt.float32, kind="ExternalOutput").ap()
    build(nc, *aps, out)
    got = run_spmd(nc, [arrays], core_ids=[0]).results[0]["out"]
    return got.reshape(NC, B, TC, D).transpose(1, 0, 2, 3).reshape(B, T, D)
```

```python
from contextlib import ExitStack

import concourse.bass as bass
from concourse import mybir

F32 = mybir.dt.float32
BF16 = mybir.dt.bfloat16
U32 = mybir.dt.uint32
ALU = mybir.AluOpType
ACT = mybir.ActivationFunctionType
X = mybir.AxisListType.X

P = 128
B, T, D = 4, 256, 128
TC = P // B
NC = T // TC
E1, E2 = 8, 4
HEADS, HD = 16, 8
G = 4
HG = HEADS // G
M_ZERO = 32
EPS = 1.1920929e-07
NEG = -1e30
FLT_MAX = 3.4028234663852886e38

REC = [("W_z", P), ("W_r", P), ("W", P), ("U_z", P), ("U_r", P), ("U", P), ("C_z", P), ("C_r", P), ("C", P)]
VEC = [("b_z", 1), ("b_r", 1), ("b", 1), ("n1", 1), ("n2", 1), ("cond", B), ("rbias", E1), ("qn", HD), ("kn", HD)]
CST = [("ident", P), ("inv", NC * TC), ("head_f", HEADS), ("head_p", HG), ("pick_t", TC), ("count8", 8),
       ("mask", (2 * NC - 1) * TC)]
MIX = [("rw_x", E1), ("rw_c", E1), ("w1", 2 * P), ("w3", 2 * P), ("w2", 2 * P), ("up", E1 * P), ("down", E1 * P)]
FFN = [("wq", P), ("wk", P), ("wv", P), ("wo", P),
       ("gate", E2), ("e0_up", 2 * P), ("e1_w1", 2 * P), ("e1_w2", 2 * P), ("l1", 2 * P), ("e3_down", P),
       ("e0_down", 2 * P), ("e1_down", 2 * P), ("l2", 4 * P), ("l3", 4 * P), ("l4", 2 * P),
       ("e3_up", 2 * P), ("e3_out", 2 * P)]


def columns(table):
    at, found = 0, {}
    for name, width in table:
        found[name] = (at, at + width)
        at += width
    return found, at


def build(nc, xT, rec, vec, cst, mix, ffn, out):
    with ExitStack() as ctx:
        def sb(name, *shape, dt=F32):
            return ctx.enter_context(nc.sbuf_tensor(name, [P, *shape], dt))

        def bank(name):
            return ctx.enter_context(nc.psum_tensor(name, [P, 512], F32))

        def sem(name):
            return ctx.enter_context(nc.semaphore(name))

        x_sb = sb("x_sb", (NC + 1) * P)
        packs = {}
        for name, table in (("rec", REC), ("vec", VEC), ("cst", CST), ("mix", MIX), ("ffn", FFN)):
            found, width = columns(table)
            packs[name] = (sb(name + "_sb", width), found)

        def part(pack, name, lo=0, n=None):
            t, found = packs[pack]
            a, b = found[name]
            return t[:, a + lo:(b if n is None else a + lo + n)]

        ident = part("cst", "ident")
        u_half = sb("u_half", 4, P)
        gate_bias = sb("gate_bias", 3, B)
        cond_rep = sb("cond_rep", B, TC)
        route_c = sb("route_c", E1)
        qk_scale = sb("qk_scale", P)
        mask_bf = sb("mask_bf", (2 * NC - 1) * TC, dt=BF16)
        ident_bf = sb("ident_bf", P, dt=BF16)
        e_const = sb("e_const", 8)
        neg_half = sb("neg_half", 2 * HEADS)

        h2 = sb("h2", 2, B)
        tz, tr, th = sb("tz", 2, B), sb("tr", 2, B), sb("th", 2, B)
        g_in, kept, new = sb("g_in", 2, B), sb("kept", 2, B), sb("new", 2, B)
        idle = sb("idle", 384, dt=BF16)
        run = sb("run", B, TC)

        mean = sb("mean", B, TC)
        x1 = sb("x1", P)
        x1t = sb("x1t", P)
        sm = sb("sm", 64)
        ix1, ix2 = sb("ix1", 8, dt=U32), sb("ix2", 8, dt=U32)
        comb = sb("comb", E1)
        th_sh, s_a, s_h = sb("th_sh", 2, P), sb("s_a", 2, P), sb("s_h", 2, P)
        ge = sb("ge", E1, P)
        acc = sb("acc", P)
        x2 = sb("x2", P)
        sq = sb("sq", 2 * P)
        rs = sb("rs", 8)
        hn, hn_f = sb("hn", P), sb("hn_f", P)
        ss_h, r_h = sb("ss_h", 2 * HEADS), sb("r_h", 2 * HEADS)
        q_n, q_s, k_n = sb("q_n", P), sb("q_s", P), sb("k_n", P)
        v_n, k_f, q_f = sb("v_n", P), sb("k_f", P), sb("q_f", B, TC)
        q_m = sb("q_m", B, HEADS, TC)
        k_c = sb("k_c", NC * P)
        v_c = sb("v_c", NC * G * P)
        nmax, psum_r = sb("nmax", 16), sb("psum_r", 16)
        p_e = sb("p_e", 2, NC * P)
        p_t = sb("p_t", 2, NC * P)
        inv_sum = sb("inv_sum", 16)
        ao_m = sb("ao_m", B, G, 32)
        ao_f = sb("ao_f", P)
        xn, xn_f = sb("xn", P), sb("xn_f", P)
        x3 = sb("x3", P)
        sm2 = sb("sm2", 96)
        sq2 = sb("sq2", P)
        rs2 = sb("rs2", 8)
        wts = sb("wts", 8)
        gf = sb("gf", 11, P)
        th_e, e_a, e_h = sb("th_e", 2, P), sb("e_a", 2, P), sb("e_h", 2, P)
        base = sb("base", P)
        fin = sb("fin", P)

        bk_r, bk_z, bk_h = bank("bk_r"), bank("bk_z"), bank("bk_h")
        b0, b1, b2, b3, b4 = (bank(f"b{i}") for i in range(5))

        in_rec, in_x, in_mix, in_ffn = sem("in_rec"), sem("in_x"), sem("in_mix"), sem("in_ffn")
        u_ready, rec_ps, gb_ready, cr_ready = sem("u_ready"), sem("rec_ps"), sem("gb_ready"), sem("cr_ready")
        rc_ps, dve_setup, pool_setup, filled = sem("rc_ps"), sem("dve_setup"), sem("pool_setup"), sem("filled")
        idle_ready = sem("idle_ready")
        parts_go, out_done = sem("parts_go"), sem("out_done")
        begun = {n: sem("begun_" + n) for n in ("pe", "act", "dve", "sp")}

        names = """r_acc z_acc h_acc r_act z_act h_act g_ready kept_ready new_ready h_ready run_ready left""".split()
        R = [{n: sem(f"{n}_{k}") for n in names} for k in ("even", "odd")]
        cleared = sem("cleared")

        names = """mean_ready x1_ready lg_ps nl_ready sig_e dchain dchain2 e_ready comb_ready x1t_ps x1t_ready sh_ps sh_th sa_ready
            sh_ready up_ps ge_ready shd_ps dn_ps acc_ready x2_ready ms_ready r1_ready hn_ready hn_ps hnf_ready qk_ps v_ps
            sq_ready ssh_ready rh_ready qn_ready qs_ready kn_ready qt_ps kt_ps qm_ready qf_ready kf_ready vn_ready kc_ready vc_ready
            sc_ps nmax_ready pe_ready pt_ps pt_ready pv_ps inv_ready aom_ready ao_ps aof_ready wo_ps x3_ready
            ms2_ready r2_ready xn_ready xn_ps xnf_ready gt_ps ge_nl ge_e wts_ready hid_ps hid_ready e1_ps
            e1_th ea_ready eh_ready o_ps moe_ready base_ready x3c_ready fin_free parts_done""".split()
        S = {n: sem(n) for n in names}

        def span(sems):
            nums = sorted(s.num for s in sems.values())
            assert nums == list(range(nums[0], nums[0] + len(nums)))
            return range(nums[0], nums[-1] + 1)

        block = ctx.enter_context(nc.Block())

        def pacer(*programs):
            due = [next(p, None) for p in programs]

            def advance(step):
                for n, p in enumerate(programs):
                    while due[n] is not None and due[n] <= step:
                        due[n] = next(p, None)
            return advance

        def merge(*programs):
            advance = pacer(*programs)
            for t in range(2 * 10 * TC):
                advance(t / 20)
            advance(ALL)

        LOOPS = ((2, 2 + NC // 2, NC // 2), (2 + NC // 2, NC, NC - 2))

        def begin(engine, name, go, n):
            engine.wait_ge(go, n)
            engine.sem_inc(begun[name], 1)

        def enter(engine, name, t, c):
            if t == 0 and not (isinstance(c, int) and c == 0):
                begin(engine, name, parts_go, c)

        def leave(engine, t, before):
            if t == 1 and before:
                engine.drain().then_inc(before["left"], 1)
            if t == TC - 1:
                engine.drain().then_inc(S["parts_done"], 1)

        def chunks(engine, name, one_pass):
            def both(c, k, nk):
                begin(engine, name, cleared, c - 1)
                one_pass(c, R[k], R[1 - k], nk)
            one_pass(0, R[0], None, None)
            one_pass(1, R[1], R[0], None)
            for lo, hi, nk in LOOPS:
                with engine.Fori(lo, hi - 1, 2) as c:
                    both(c, 0, nk)
                    both(c + 1, 1, nk)

        ALL = 1e9
        WINDOW, WINDOW_BOTH = 1000, 1300

        def bcast(ap, axis, shape):
            return ap.unsqueeze(axis).to_broadcast(shape)

        def tile_cols(tile):
            return bass.ds(tile * P, P)

        @block.tensor
        def _(pe):
            streamed = [0]
            window = [WINDOW]

            def keep_clock(bk):
                while streamed[0] < window[0]:
                    n = min(3 * P, window[0] - streamed[0])
                    mm(bk[:, P:P + n], idle[:, 0:P], idle[:, 0:n], start=False)
                streamed[0] = 0

            def table_load():
                streamed[0] -= 3000

            def mm(o, w, r, start=True, stop=True):
                streamed[0] += o.free_size() * w.shape[0] * (4 if w.dtype == F32 else 1) // P
                return pe.matmul(o, w, r, start=start, stop=stop, skip_group_check=True)

            def transpose(o, x):
                streamed[0] += P
                return pe.transpose(o, x, ident)

            def fill(gate, bk, chunk):
                mm(bk[:, 0:P], part("rec", ("W_z", "W_r", "W")[gate]), x_sb[:, tile_cols(chunk)])
                return mm(bk[:, 0:P], ident, bcast(gate_bias[:, gate, :], 2, [P, B, TC]), start=False)

            def at(bk, t):
                return bk[:, t:P:TC]

            def gru(advance, c, R, before):
                streamed[0] = 0
                for t in range(TC):
                    if t == 0 and not before:
                        mm(at(bk_r, t), u_half[:, 1, :], h2[:, 0, :], start=False).then_inc(R["r_acc"], 1)
                    else:
                        last, n = (R, t) if t else (before, TC)
                        pe.wait_ge(last["kept_ready"], n)
                        mm(at(bk_r, t), u_half[:, 3, :], kept[:, t % 2, :], start=False)
                        advance(t - 0.4)
                        keep_clock(bk_r)
                        pe.wait_ge(last["new_ready"], n)
                        mm(at(bk_r, t), u_half[:, 1, :], new[:, t % 2, :], start=False).then_inc(R["r_acc"], 1)
                        pe.wait_ge(last["h_ready"], n)
                    mm(at(bk_z, t), u_half[:, 0, :], h2[:, t % 2, :], start=False).then_inc(R["z_acc"], 1)
                    if t == 0:
                        if before:
                            pe.wait_ge(before["h_act"], TC)
                        fill(2, bk_h, c)
                    enter(pe, "pe", t, c)
                    advance(t + 0.1 if t < TC - 1 else ALL)
                    leave(pe, t, before)
                    keep_clock(bk_h)
                    pe.wait_ge(R["g_ready"], t + 1)
                    mm(at(bk_h, t), u_half[:, 2, :], g_in[:, t % 2, :], start=False).then_inc(R["h_acc"], 1)
                pe.wait_ge(R["r_act"], TC)
                fill(1, bk_r, c + 1)
                pe.wait_ge(R["z_act"], TC)
                fill(0, bk_z, c + 1)

            def setup():
                yield 20.1
                pe.wait_ge(in_mix, 16)
                pe.wait_ge(cr_ready, 1)
                mm(b1[:, 0:E1], cond_rep[:, :, :], part("mix", "rw_c")).then_inc(rc_ps, 1)

            def part1(i):
                yield 0.6
                pe.wait_ge(S["x1_ready"], 1)
                mm(b0[:, 0:E1], x1[:, :], part("mix", "rw_x")).then_inc(S["lg_ps"], 1)
                transpose(b1[:, 0:P], x1[:, :]).then_inc(S["x1t_ps"], 1)
                for e in range(E1):
                    yield 1.1 + e / 2
                    if e < 2:
                        pe.wait_ge(S[("nl_ready", "x1t_ready")[e]], 1)
                    else:
                        pe.wait_ge(S["ge_ready"], e - 1)
                    mm((b0, b1)[e % 2][:, 0:P], part("mix", "up", e * P, P), x1[:, :]).then_inc(S["up_ps"], 1)
                for j, bk in enumerate((b0, b1)):
                    yield 5.1 + j
                    pe.wait_ge(S["ge_ready"], E1 - 1 + j)
                    mm(bk[:, 0:P], part("mix", "w1", j * P, P), x1[:, :])
                    yield 5.6 + j
                    mm(bk[:, P:2 * P], part("mix", "w3", j * P, P), x1[:, :]).then_inc(S["sh_ps"], 1)
                yield 7.6
                pe.wait_ge(S["sh_ready"], 2)
                mm(b0[:, 0:P], s_h[:, 0, :], part("mix", "w2", 0, P), stop=False)
                yield 8.1
                mm(b0[:, 0:P], s_h[:, 1, :], part("mix", "w2", P, P), start=False).then_inc(S["shd_ps"], 1)
                for e in range(E1):
                    yield 8.6 + e / 2
                    if e == 0:
                        pe.wait_ge(S["ge_ready"], E1)
                    else:
                        pe.wait_ge(S["acc_ready"], e)
                    mm((b1, b0)[e % 2][:, 0:P], ge[:, e, :], part("mix", "down", e * P, P)).then_inc(S["dn_ps"], 1)
                yield 14.6
                pe.wait_ge(S["hn_ready"], 1)
                transpose(b0[:, 0:P], hn[:, :]).then_inc(S["hn_ps"], 1)
                yield 15.1
                pe.wait_ge(S["hnf_ready"], 1)
                mm(b1[:, 0:P], hn_f[:, :], part("ffn", "wq"))
                mm(b1[:, P:2 * P], hn_f[:, :], part("ffn", "wk")).then_inc(S["qk_ps"], 1)
                yield 15.6
                mm(b0[:, 0:P], hn_f[:, :], part("ffn", "wv")).then_inc(S["v_ps"], 1)
                yield 20.6
                pe.wait_ge(S["vn_ready"], 1)
                pe.wait_ge(S["kn_ready"], 1)
                transpose(b0[:, 0:P], k_n[:, :]).then_inc(S["kt_ps"], 1)
                yield 21.1
                pe.wait_ge(S["qs_ready"], 1)
                transpose(b1[:, 0:P], q_s[:, :]).then_inc(S["qt_ps"], 1)

            def part2(i, nk):
                keys = nk * TC
                ao = b4[:, :].rearrange("p (b g f) -> p b g f", b=B, g=G)
                rounds = (nk + 3) // 4

                def scores(m):
                    if m == 0:
                        pe.wait_ge(S["kc_ready"], 1)
                        pe.wait_ge(S["qm_ready"], 1)
                    else:
                        pe.wait_ge(S["pe_ready"], 2 * m)
                    for n in (2 * m, 2 * m + 1):
                        g, b = n // B, n % B
                        cols = slice((n % 2) * keys, (n % 2 + 1) * keys)
                        mm(b2[:, cols], q_m[:, b, g * HG:(g + 1) * HG, :],
                           k_c[:, :].rearrange("p (i b t) -> p i b t", b=B, t=TC)[:, 0:nk, b, :], stop=False)
                        last = mm(b2[:, cols], ident_bf[:, :], mask_bf[:, bass.ds((NC - 1 - i) * TC, keys)], start=False)
                    last.then_inc(S["sc_ps"], 1)

                def turn(g, n):
                    pe.wait_ge(S["pe_ready"], B * (g + 1))
                    if g or n:
                        pe.wait_ge(S["pt_ready"], g * (nk // 2) + 2 * n)
                    for c in range(4 * n, min(4 * n + 4, nk)):
                        last = transpose(b3[:, (c % 4) * P:(c % 4 + 1) * P], p_e[:, g % 2, c * P:(c + 1) * P])
                    last.then_inc(S["pt_ps"], 1)

                def values(g, c):
                    if g == 0 and c == 0:
                        pe.wait_ge(S["vc_ready"], B)
                    pe.wait_ge(S["pt_ready"], g * (nk // 2) + c // 2 + 1)
                    last = mm(ao[:, :, g, :], p_t[:, g % 2, c * P:(c + 1) * P],
                              v_c[:, (c * G + g) * P:(c * G + g + 1) * P], start=(c == 0), stop=(c == nk - 1))
                    if c == nk - 1:
                        last.then_inc(S["pv_ps"], 1)

                for g in range(G + 1):
                    at = 4.6 + 3 * g
                    if g < G:
                        yield at
                        scores(2 * g)
                    if g == 0:
                        yield at + 1.0
                        table_load()
                    if g:
                        yield at + 0.5
                        turn(g - 1, 0)
                        yield at + 1.0
                        values(g - 1, 0)
                        values(g - 1, 1)
                    if g < G:
                        yield at + 1.5
                        scores(2 * g + 1)
                    if g:
                        yield at + 2.0
                        values(g - 1, 2)
                        values(g - 1, 3)
                        if rounds == 2:
                            turn(g - 1, 1)
                            yield at + 2.5
                            values(g - 1, 4)
                            values(g - 1, 5)
                            yield at + 3.0
                            for k in range(6, nk):
                                values(g - 1, k)
                yield 21.1
                pe.wait_ge(S["aom_ready"], HG)
                for b in range(B):
                    last = mm(b2[:, b * TC:(b + 1) * TC], ao_m[:, b, :, :], part("cst", "pick_t"))
                last.then_inc(S["ao_ps"], 1)
                yield 21.6
                pe.wait_ge(S["aof_ready"], 1)
                mm(b3[:, 0:P], ao_f[:, :], part("ffn", "wo")).then_inc(S["wo_ps"], 1)
                yield 23.6
                pe.wait_ge(S["xn_ready"], 1)
                transpose(b2[:, 0:P], xn[:, :]).then_inc(S["xn_ps"], 1)
                yield 24.1
                pe.wait_ge(S["xnf_ready"], 1)
                mm(b4[:, 0:E2], xn_f[:, :], part("ffn", "gate")).then_inc(S["gt_ps"], 1)

                def f(name, k=0):
                    return part("ffn", name, k * P, P)

                def hidden(n, pieces):
                    if n >= 2:
                        pe.wait_ge(S["hid_ready"], n - 1)
                    for k, (w, x) in enumerate(pieces):
                        last = mm((b2, b3)[n % 2][:, 0:P], w, x, start=(k == 0), stop=(k == len(pieces) - 1))
                    last.then_inc(S["hid_ps"], 1)

                def gated(j):
                    mm(b4[:, 0:P], f("e1_w1", j), xn_f[:, :])
                    mm(b4[:, P:2 * P], f("e1_w2", j), xn_f[:, :]).then_inc(S["e1_ps"], 1)

                def result(bk, name, h):
                    mm(bk[:, 0:P], h[0], f(name, 0), stop=False)
                    mm(bk[:, 0:P], h[1], f(name, 1), start=False).then_inc(S["o_ps"], 1)

                hidden(0, [(f("e0_up", 0), xn_f[:, :])])
                yield 24.6
                table_load()
                hidden(1, [(f("e0_up", 1), xn_f[:, :])])
                hidden(2, [(f("l1", 0), xn_f[:, :])])
                yield 25.1
                hidden(3, [(f("l1", 1), xn_f[:, :])])
                pe.wait_ge(S["ge_nl"], 1)
                gated(0)
                yield 25.6
                hidden(4, [(f("e3_down"), xn_f[:, :])])
                yield 26.1
                pe.wait_ge(S["hid_ready"], 4)
                hidden(5, [(f("l2", 0), gf[:, 2, :]), (f("l2", 1), gf[:, 3, :])])
                pe.wait_ge(S["eh_ready"], 1)
                gated(1)
                yield 26.6
                hidden(6, [(f("l2", 2), gf[:, 2, :]), (f("l2", 3), gf[:, 3, :])])
                yield 27.1
                hidden(7, [(f("e3_up", 0), gf[:, 4, :])])
                hidden(8, [(f("e3_up", 1), gf[:, 4, :])])
                yield 27.6
                pe.wait_ge(S["hid_ready"], 7)
                hidden(9, [(f("l3", 0), gf[:, 5, :]), (f("l3", 1), gf[:, 6, :])])
                pe.wait_ge(S["eh_ready"], 2)
                result(b4, "e0_down", (gf[:, 0, :], gf[:, 1, :]))
                yield 28.1
                hidden(10, [(f("l3", 2), gf[:, 5, :]), (f("l3", 3), gf[:, 6, :])])
                yield 28.6
                pe.wait_ge(S["hid_ready"], 10)
                result(b3, "e1_down", (e_h[:, 0, :], e_h[:, 1, :]))
                yield 29.1
                pe.wait_ge(S["hid_ready"], 11)
                result(b2, "e3_out", (gf[:, 7, :], gf[:, 8, :]))
                yield 29.6
                pe.wait_ge(S["moe_ready"], 1)
                result(b4, "l4", (gf[:, 9, :], gf[:, 10, :]))

            pe.wait_ge(idle_ready, 1)
            for _ in range(40):
                mm(bk_r[:, 0:3 * P], idle[:, 0:P], idle[:, :])
            pe.wait_ge(in_rec, 3 * 16)
            for gate in range(3):
                last = mm(b0[:, gate * B:(gate + 1) * B], part("rec", ("C_z", "C_r", "C")[gate]), part("vec", "cond"))
            last.then_inc(rec_ps, 1)
            pe.wait_ge(in_x, 16)
            pe.wait_ge(gb_ready, 3)
            fill(0, bk_z, 0)
            fill(1, bk_r, 0)
            pe.wait_ge(u_ready, 5)

            def one_pass(c, R, before, nk):
                if nk:
                    window[0] = WINDOW_BOTH
                    gru(pacer(part1(c - 1), part2(c - 2, nk)), c, R, before)
                else:
                    gru(pacer(part1(0) if before else setup()), c, R, before)
            window = [WINDOW]
            chunks(pe, "pe", one_pass)
            begin(pe, "pe", parts_go, NC)
            merge(part1(NC - 1), part2(NC - 2, NC))
            pe.drain().then_inc(S["parts_done"], 1)
            begin(pe, "pe", parts_go, NC + 1)
            merge(part2(NC - 1, NC))

        @block.scalar
        def _(act):
            def at(bk, t):
                return bk[:, t:P:TC]

            def gru(advance, c, R, before):
                for t in range(TC):
                    act.wait_ge(R["r_acc"], t + 1)
                    act.activation(tr[:, t % 2, :], at(bk_r, t), ACT.Tanh, scale=0.5).then_inc(R["r_act"], 1)
                    act.wait_ge(R["z_acc"], t + 1)
                    act.activation(tz[:, t % 2, :], at(bk_z, t), ACT.Tanh, scale=0.5).then_inc(R["z_act"], 1)
                    enter(act, "act", t, c)
                    advance(t + 0.3 if t < TC - 1 else ALL)
                    leave(act, t, before)
                    act.wait_ge(R["h_acc"], t + 1)
                    act.activation(th[:, t % 2, :], at(bk_h, t), ACT.Tanh).then_inc(R["h_act"], 1)
                    if t < TC - 1:
                        advance(t + 0.7)

            def part1(i):
                yield 1.3
                act.wait_ge(S["base_ready"], 1)
                act.wait_ge(S["x1t_ps"], 1)
                act.copy(x1t[:, :], b1[:, 0:P]).then_inc(S["x1t_ready"], 1)
                for e in range(E1):
                    yield 1.3 + e // 2 + 0.4 * (e % 2)
                    act.wait_ge(S["up_ps"], e + 1)
                    act.activation(ge[:, e, :], (b0, b1)[e % 2][:, 0:P], ACT.Gelu).then_inc(S["ge_ready"], 1)
                for j, bk in enumerate((b0, b1)):
                    yield 5.7 + j
                    act.wait_ge(S["sh_ps"], j + 1)
                    act.activation(th_sh[:, j, :], bk[:, 0:P], ACT.Tanh, scale=0.5).then_inc(S["sh_th"], 1)
                yield 14.7
                act.wait_ge(S["hn_ps"], 1)
                act.copy(hn_f[:, :], b0[:, 0:P]).then_inc(S["hnf_ready"], 1)
                yield 15.7
                act.wait_ge(S["qk_ps"], 1)
                act.activation(sq[:, :], b1[:, 0:2 * P], ACT.Square).then_inc(S["sq_ready"], 1)
                yield 16.3
                act.wait_ge(S["v_ps"], 1)
                act.copy(v_n[:, :], b0[:, 0:P]).then_inc(S["vn_ready"], 1)
                yield 20.7
                act.wait_ge(S["kt_ps"], 1)
                act.copy(k_f[:, :], b0[:, 0:P]).then_inc(S["kf_ready"], 1)
                yield 21.3
                act.wait_ge(S["qt_ps"], 1)
                act.copy(q_f[:, :, :], b1[:, 0:P].rearrange("p (b t) -> p b t", b=B)).then_inc(S["qf_ready"], 1)

            def part2(i, nk):
                keys = nk * TC
                rounds = (nk + 3) // 4
                yield 0.7
                act.copy(k_c[:, tile_cols(i)], k_f[:, :]).then_inc(S["kc_ready"], 1)

                def cache_v(b):
                    rows = slice(TC * b, TC * (b + 1))
                    act.copy(v_c[rows, bass.ds(i * (G * P), G * P)].rearrange("p (g b f) -> p g b f", g=G, b=B)[:, :, b, :],
                             v_n[rows, :].rearrange("p (g f) -> p g f", g=G)).then_inc(S["vc_ready"], 1)

                def exps(n):
                    g, b = n // B, n % B
                    act.wait_ge(S["nmax_ready"], n // 2 + 1)
                    if b == 0 and g >= 2:
                        act.wait_ge(S["pt_ps"], (g - 1) * rounds)
                    o = p_e[:, g % 2, :].rearrange("p (c b t) -> p c b t", b=B, t=TC)[:, 0:nk, b, :]
                    cols = slice((n % 2) * keys, (n % 2 + 1) * keys)
                    act.activation(o, b2[:, cols].rearrange("p (c t) -> p c t", t=TC), ACT.Exp,
                                   bias=nmax[:, n:n + 1],
                                   accum_out=psum_r[:, b * G + g:b * G + g + 1]).then_inc(S["pe_ready"], 1)

                def spread(g, n, m):
                    act.wait_ge(S["pt_ps"], g * rounds + n + 1)
                    if g >= 2 and n == 0 and m == 0:
                        act.wait_ge(S["pv_ps"], g - 1)
                    if 4 * n + 2 * m < nk:
                        lo = n * 512 + m * 256
                        act.copy(p_t[:, g % 2, lo:lo + 256], b3[:, m * 256:m * 256 + 256]).then_inc(S["pt_ready"], 1)

                for g in range(G + 1):
                    at = 5.3 + 3 * g
                    yield at
                    if g < G:
                        exps(4 * g)
                    if g:
                        spread(g - 1, 0, 0)
                    yield at + 0.4
                    if g < G:
                        exps(4 * g + 1)
                    if g == 0:
                        yield at + 0.7
                        cache_v(0)
                        cache_v(1)
                    else:
                        spread(g - 1, 0, 1)
                    if g < G:
                        yield at + 1.4
                        exps(4 * g + 2)
                    if g and rounds == 2:
                        yield at + 1.4
                        spread(g - 1, 1, 0)
                    if g < G:
                        yield at + 2.0
                        exps(4 * g + 3)
                    if g == 0:
                        yield at + 2.4
                        cache_v(2)
                        cache_v(3)
                    if g and rounds == 2:
                        yield at + 2.0
                        spread(g - 1, 1, 1)
                yield 21.3
                act.wait_ge(S["ao_ps"], 1)
                act.copy(ao_f[:, :], b2[:, 0:P]).then_inc(S["aof_ready"], 1)
                yield 23.7
                act.wait_ge(S["xn_ps"], 1)
                act.copy(xn_f[:, :], b2[:, 0:P]).then_inc(S["xnf_ready"], 1)

                def gelu(n):
                    act.wait_ge(S["hid_ps"], n + 1)
                    act.activation(gf[:, n, :], (b2, b3)[n % 2][:, 0:P], ACT.Gelu).then_inc(S["hid_ready"], 1)

                def tanh(j):
                    act.wait_ge(S["e1_ps"], j + 1)
                    act.activation(th_e[:, j, :], b4[:, 0:P], ACT.Tanh, scale=0.5).then_inc(S["e1_th"], 1)

                yield 24.3
                gelu(0)
                yield 24.7
                gelu(1)
                gelu(2)
                yield 25.3
                gelu(3)
                tanh(0)
                yield 25.7
                gelu(4)
                yield 26.3
                gelu(5)
                tanh(1)
                yield 26.7
                gelu(6)
                yield 27.3
                gelu(7)
                gelu(8)
                yield 27.7
                gelu(9)
                yield 28.3
                gelu(10)

            act.preload_act_table(ACT.Gelu)

            def one_pass(c, R, before, nk):
                if nk:
                    gru(pacer(part1(c - 1), part2(c - 2, nk)), c, R, before)
                else:
                    gru(pacer(part1(0)) if before else pacer(), c, R, before)
            chunks(act, "act", one_pass)
            begin(act, "act", parts_go, NC)
            merge(part1(NC - 1), part2(NC - 2, NC))
            act.drain().then_inc(S["parts_done"], 1)
            begin(act, "act", parts_go, NC + 1)
            merge(part2(NC - 1, NC))

        @block.vector
        def _(dve):
            def gru(advance, c, R, before):
                def add_run(t):
                    dve.wait_ge(R["h_ready"], t + 1)
                    if t >= 1:
                        dve.wait_ge(R["run_ready"], t)
                    prev = (t - 1) % TC
                    dve.tensor_tensor(run[:, :, t], run[:, :, prev], h2[:, (t + 1) % 2, :],
                                      ALU.add).then_inc(R["run_ready"], 1)

                for t in range(TC):
                    h, nxt = h2[:, t % 2, :], (t + 1) % 2
                    dve.wait_ge(R["r_act"], t + 1)
                    if t >= 1:
                        dve.wait_ge(R["h_ready"], t)
                    elif before:
                        dve.wait_ge(before["h_ready"], TC)
                    dve.scalar_tensor_tensor(g_in[:, t % 2, :], tr[:, t % 2, :], 1.0, h, ALU.add,
                                             ALU.mult).then_inc(R["g_ready"], 1)
                    enter(dve, "dve", t, c)
                    advance(t + 0.2)
                    if t >= 1:
                        add_run(t - 1)
                    dve.wait_ge(R["z_act"], t + 1)
                    dve.scalar_tensor_tensor(kept[:, nxt, :], tz[:, t % 2, :], 1.0, h, ALU.subtract,
                                             ALU.mult).then_inc(R["kept_ready"], 1)
                    advance(t + 0.4 if t < TC - 1 else ALL)
                    leave(dve, t, before)
                    dve.wait_ge(R["h_act"], t + 1)
                    dve.scalar_tensor_tensor(new[:, nxt, :], tz[:, t % 2, :], 1.0, th[:, t % 2, :], ALU.add,
                                             ALU.mult).then_inc(R["new_ready"], 1)
                    dve.wait_ge(R["new_ready"], t + 1)
                    dve.scalar_tensor_tensor(h2[:, nxt, :], kept[:, nxt, :], -0.5, new[:, nxt, :], ALU.mult,
                                             ALU.add).then_inc(R["h_ready"], 1)
                    if t < TC - 1:
                        advance(t + 0.8)
                add_run(TC - 1)

            def chained(name):
                count = [0]

                def step(ins):
                    count[0] += 1
                    ins.then_inc(S[name], 1)

                def after():
                    dve.wait_ge(S[name], count[0])
                return step, after

            count8 = part("cst", "count8")

            def setup():
                yield 15.8
                dve.wait_ge(in_ffn, 16)
                for lo, hi, w in (("wq", "wv", "n1"), ("gate", "e3_down", "n2")):
                    t, found = packs["ffn"]
                    cols = t[:, found[lo][0]:found[hi][1]]
                    dve.tensor_scalar(cols, cols, part("vec", w), None, ALU.mult).then_inc(dve_setup, 1)
                    yield 17.8
                yield 21.4
                dve.wait_ge(rc_ps, 1)
                dve.tensor_copy(route_c[:, :], b1[:, 0:E1]).then_inc(dve_setup, 1)

            def part1(i, last_run, alone=False):
                step, after = chained("dchain")
                yield 0.2
                if alone:
                    dve.sem_inc(S["base_ready"], 1)
                dve.wait_ge(last_run["run_ready"], TC)
                inv = part("cst", "inv").rearrange("p (c t) -> p c t", t=TC)
                dve.tensor_tensor(mean[:, :, :], run[:, :, :],
                                  inv[:, bass.ds(i, 1), :].to_broadcast([P, B, TC]), ALU.mult).then_inc(S["mean_ready"], 1)
                yield 0.4
                dve.wait_ge(S["mean_ready"], 1)
                dve.tensor_tensor(x1[:, :], mean[:, :, :].rearrange("p b t -> p (b t)"), x_sb[:, tile_cols(i)],
                                  ALU.add).then_inc(S["x1_ready"], 1)
                nl, e1, s, sel, mx, first, mask, q = (sm[:, 8 * k:8 * k + 8] for k in range(8))
                yield 0.8
                dve.wait_ge(S["lg_ps"], 1)
                dve.scalar_tensor_tensor(nl, b0[:, 0:E1], -1.0, route_c[:, :], ALU.mult,
                                         ALU.subtract).then_inc(S["nl_ready"], 1)

                def swiglu(j, bk):
                    yield 5.8 + j
                    dve.wait_ge(S["sh_th"], j + 1)
                    dve.scalar_tensor_tensor(s_a[:, j, :], th_sh[:, j, :], 1.0, bk[:, 0:P], ALU.add,
                                             ALU.mult).then_inc(S["sa_ready"], 1)
                    yield 6.2 + j
                    dve.wait_ge(S["sa_ready"], j + 1)
                    dve.tensor_tensor(s_h[:, j, :], s_a[:, j, :], bk[:, P:2 * P], ALU.mult).then_inc(S["sh_ready"], 1)

                yield 3.2
                dve.wait_ge(S["sig_e"], 1)
                step(dve.tensor_scalar(e1, e1, 1.0, None, ALU.add))
                yield 3.4
                after()
                step(dve.reciprocal(s, e1))
                yield 3.8
                after()
                step(dve.tensor_tensor(sel, s, part("vec", "rbias"), ALU.add))
                yield 4.2
                after()
                step(dve.max(mx, sel))
                yield 4.4
                after()
                step(dve.max_index(ix1[:, :], mx, sel))
                yield 4.8
                after()
                step(dve.tensor_scalar(first, count8, ix1[:, 0:1], None, ALU.is_equal))
                yield 5.2
                after()
                step(dve.scalar_tensor_tensor(mask, count8, ix1[:, 1:2], first, ALU.is_equal, ALU.add))
                yield 5.4
                after()
                den, ok = q[:, 0:1], q[:, 1:2]
                step(dve.scalar_tensor_tensor(sel, mask, 1.0, s, ALU.mult, ALU.mult, accum_out=den))
                yield from swiglu(0, b0)
                yield 6.2
                after()
                step(dve.tensor_scalar(ok, den, 1e-9, None, ALU.is_gt))
                step(dve.tensor_scalar(q[:, 2:3], den, 1e-9, None, ALU.add))
                yield 6.4
                after()
                step(dve.reciprocal(q[:, 3:4], q[:, 2:3]))
                step(dve.tensor_scalar(q[:, 4:5], ok, -0.5, 0.5, ALU.mult, ALU.add))
                yield from swiglu(1, b1)
                after()
                step(dve.tensor_tensor(q[:, 5:6], q[:, 3:4], ok, ALU.mult))
                yield 7.4
                step(dve.tensor_scalar(first, mask, q[:, 4:5], None, ALU.mult))
                yield 7.8
                after()
                dve.scalar_tensor_tensor(comb[:, :], sel, q[:, 5:6], first, ALU.mult,
                                         ALU.add).then_inc(S["comb_ready"], 1)
                yield 8.4
                dve.wait_ge(S["shd_ps"], 1)
                dve.tensor_scalar(acc[:, :], b0[:, 0:P], 0.5, None, ALU.mult).then_inc(S["acc_ready"], 1)
                dve.wait_ge(S["comb_ready"], 1)
                for e in range(E1):
                    yield 8.8 + e / 2
                    dve.wait_ge(S["dn_ps"], e + 1)
                    dve.wait_ge(S["acc_ready"], e + 1)
                    dve.scalar_tensor_tensor(acc[:, :], (b1, b0)[e % 2][:, 0:P], comb[:, e:e + 1], acc[:, :], ALU.mult,
                                             ALU.add).then_inc(S["acc_ready"], 1)
                yield 12.8
                dve.wait_ge(S["acc_ready"], E1 + 1)
                dve.wait_ge(S["base_ready"], 1)
                dve.tensor_scalar(x2[:, :], acc[:, :], 1.0 / 3.0, None, ALU.mult).then_inc(S["x2_ready"], 1)
                yield 13.2
                dve.wait_ge(S["x2_ready"], 1)
                step(dve.scalar_tensor_tensor(acc[:, :], x2[:, :], 1.0, x2[:, :], ALU.mult, ALU.mult,
                                              accum_out=rs[:, 0:1]))
                yield 13.4
                after()
                dve.tensor_scalar(rs[:, 1:2], rs[:, 0:1], 1.0 / D, EPS, ALU.mult, ALU.add).then_inc(S["ms_ready"], 1)
                yield 14.2
                dve.wait_ge(S["r1_ready"], 1)
                dve.tensor_scalar(hn[:, :], x2[:, :], rs[:, 2:3], None, ALU.mult).then_inc(S["hn_ready"], 1)
                yield 15.8
                dve.wait_ge(S["sq_ready"], 1)
                step(dve.tensor_reduce(ss_h[:, :], sq[:, :].rearrange("p (h d) -> p h d", d=HD), X, ALU.add))
                yield 16.2
                after()
                dve.tensor_scalar(ss_h[:, :], ss_h[:, :], 1.0 / HD, EPS, ALU.mult, ALU.add).then_inc(S["ssh_ready"], 1)

                def heads(ap):
                    return ap.rearrange("p (h d) -> p h d", d=HD)

                yield 19.8
                dve.wait_ge(S["rh_ready"], 1)
                dve.tensor_tensor(heads(k_n[:, :]), heads(b1[:, P:2 * P]), bcast(r_h[:, HEADS:], 2, [P, HEADS, HD]),
                                  ALU.mult).then_inc(S["kn_ready"], 1)
                yield 20.2
                dve.tensor_tensor(heads(q_n[:, :]), heads(b1[:, 0:P]), bcast(r_h[:, 0:HEADS], 2, [P, HEADS, HD]),
                                  ALU.mult).then_inc(S["qn_ready"], 1)
                yield 20.8
                dve.wait_ge(S["qn_ready"], 1)
                dve.tensor_tensor(q_s[:, :], q_n[:, :], qk_scale[:, :], ALU.mult).then_inc(S["qs_ready"], 1)

            def part2(i, nk):
                step, after = chained("dchain2")
                keys = nk * TC
                yield 0.8
                dve.tensor_copy(x3[:, :], x2[:, :]).then_inc(S["x3c_ready"], 1)
                yield 1.2
                dve.tensor_tensor(base[:, :], x2[:, :], x1t[:, :], ALU.add).then_inc(S["base_ready"], 1)
                for m in range(2 * G):
                    yield 4.8 + 1.5 * m + (0.1 if m % 2 else 0.0)
                    dve.wait_ge(S["sc_ps"], m + 1)
                    dve.tensor_reduce(nmax[:, 2 * m:2 * m + 2], b2[:, 0:2 * keys].rearrange("p (n k) -> p n k", n=2),
                                      X, ALU.max, negate=True).then_inc(S["nmax_ready"], 1)
                yield 17.2
                dve.wait_ge(S["pe_ready"], B * G)
                dve.reciprocal(inv_sum[:, :], psum_r[:, :]).then_inc(S["inv_ready"], 1)
                for h in range(HG):
                    yield (19.8, 20.2, 20.4, 20.8)[h]
                    dve.wait_ge(S["inv_ready"], 1)
                    dve.wait_ge(S["pv_ps"], G)
                    o = ao_m[:, :, :, h * HD:(h + 1) * HD].rearrange("p b g d -> p (b g) d")
                    s_ = b4[:, :].rearrange("p (n f) -> p n f", f=32)[:, :, h * HD:(h + 1) * HD]
                    dve.scalar_tensor_tensor(o, s_, part("cst", "head_p", h, 1), bcast(inv_sum[:, :], 2, [P, 16, HD]),
                                             ALU.mult, ALU.mult).then_inc(S["aom_ready"], 1)
                yield 21.8
                dve.wait_ge(S["wo_ps"], 1)
                dve.wait_ge(S["x3c_ready"], 1)
                dve.tensor_tensor(x3[:, M_ZERO:], x3[:, M_ZERO:], b3[:, M_ZERO:P], ALU.add).then_inc(S["x3_ready"], 1)
                dve.wait_ge(S["base_ready"], 1)
                dve.tensor_tensor(base[:, M_ZERO:], base[:, M_ZERO:], b3[:, M_ZERO:P], ALU.add).then_inc(S["base_ready"], 1)
                yield 22.2
                dve.wait_ge(S["x3_ready"], 1)
                step(dve.scalar_tensor_tensor(sq2[:, :], x3[:, :], 1.0, x3[:, :], ALU.mult, ALU.mult,
                                              accum_out=rs2[:, 3:4]))
                yield 22.4
                after()
                dve.tensor_scalar(rs2[:, 4:5], rs2[:, 3:4], 1.0 / D, EPS, ALU.mult, ALU.add).then_inc(S["ms2_ready"], 1)
                yield 23.4
                dve.wait_ge(S["r2_ready"], 1)
                dve.tensor_scalar(xn[:, :], x3[:, :], rs2[:, 5:6], None, ALU.mult).then_inc(S["xn_ready"], 1)

                def swiglu(j, at):
                    yield at[0]
                    dve.wait_ge(S["e1_th"], j + 1)
                    dve.scalar_tensor_tensor(e_a[:, j, :], th_e[:, j, :], 1.0, b4[:, 0:P], ALU.add,
                                             ALU.mult).then_inc(S["ea_ready"], 1)
                    yield at[1]
                    dve.wait_ge(S["ea_ready"], j + 1)
                    dve.tensor_tensor(e_h[:, j, :], e_a[:, j, :], b4[:, P:2 * P], ALU.mult).then_inc(S["eh_ready"], 1)

                lg, eq, clean, d, e_, mx, first, mask, q = (sm2[:, 8 * k:8 * k + 8] for k in range(9))
                cols = slice(0, E2)
                yield 24.2
                step(dve.memset(clean[:, cols], 0.0))
                step(dve.memset(e_, -1.0))
                yield 24.4
                dve.wait_ge(S["gt_ps"], 1)
                dve.tensor_copy(lg[:, cols], b4[:, 0:E2]).then_inc(S["ge_nl"], 1)
                yield 24.8
                dve.wait_ge(S["ge_nl"], 1)
                step(dve.tensor_tensor(eq.bitcast(U32)[:, cols], lg[:, cols], lg[:, cols], ALU.is_equal))
                yield 25.2
                after()
                step(dve.copy_predicated(clean[:, cols], eq.bitcast(U32)[:, cols], lg[:, cols]))
                yield from swiglu(0, (25.4, 25.8))
                after()
                step(dve.tensor_scalar(clean[:, cols], clean[:, cols], FLT_MAX, -FLT_MAX, ALU.min, ALU.max))
                yield 26.2
                after()
                step(dve.tensor_reduce(q[:, 0:1], clean[:, cols], X, ALU.max))
                yield 26.4
                after()
                dve.tensor_scalar(d[:, cols], clean[:, cols], q[:, 0:1], None, ALU.subtract).then_inc(S["ge_e"], 1)
                yield from swiglu(1, (26.8, 27.2))
                yield 27.4
                dve.wait_ge(S["e_ready"], 1)
                step(dve.max(mx, e_))
                step(dve.tensor_reduce(q[:, 1:2], e_[:, cols], X, ALU.add))
                yield 27.8
                after()
                step(dve.max_index(ix2[:, :], mx, e_))
                step(dve.tensor_tensor(q[:, 2:3], mx[:, 0:1], mx[:, 1:2], ALU.add))
                yield 28.2
                after()
                step(dve.tensor_scalar(first, count8, ix2[:, 0:1], None, ALU.is_equal))
                step(dve.scalar_tensor_tensor(q[:, 3:4], q[:, 1:2], 1e-8, q[:, 2:3], ALU.mult, ALU.add))
                yield 28.4
                after()
                step(dve.scalar_tensor_tensor(mask, count8, ix2[:, 1:2], first, ALU.is_equal, ALU.add))
                step(dve.reciprocal(q[:, 4:5], q[:, 3:4]))
                yield 28.8
                after()
                step(dve.scalar_tensor_tensor(wts[:, :], mask, q[:, 4:5], e_, ALU.mult, ALU.mult))
                dve.wait_ge(S["base_ready"], 2)
                dve.wait_ge(S["fin_free"], 1)
                step(dve.tensor_copy(fin[:, 0:M_ZERO], base[:, 0:M_ZERO]))
                yield 29.2
                after()
                step(dve.tensor_scalar(q[:, 5:6], wts[:, 1:2], 0.5, None, ALU.mult))
                w_of = (wts[:, 0:1], q[:, 5:6], wts[:, 3:4], wts[:, 2:3])
                for k, bk in enumerate((b4, b3, b2, b4)):
                    yield (29.4, 29.8, 30.2, 30.4)[k]
                    dve.wait_ge(S["o_ps"], k + 1)
                    if k == 0:
                        after()
                    else:
                        dve.wait_ge(S["moe_ready"], k)
                    dve.scalar_tensor_tensor((fin if k == E2 - 1 else base)[:, M_ZERO:], bk[:, M_ZERO:P], w_of[k],
                                             base[:, M_ZERO:], ALU.mult, ALU.add).then_inc(S["moe_ready"], 1)

            dve.memset(idle[:, :], 0.0).then_inc(idle_ready, 1)
            dve.memset(h2[:, :, :], 0.0).then_inc(dve_setup, 1)
            dve.memset(run[:, :, :], 0.0).then_inc(dve_setup, 1)
            dve.memset(x_sb[:, NC * P:], 0.0).then_inc(dve_setup, 1)
            dve.wait_ge(in_rec, 3 * 16)
            dve.wait_ge(rec_ps, 1)
            for gate in range(3):
                dve.tensor_scalar(gate_bias[:, gate, :], b0[:, gate * B:(gate + 1) * B],
                                  part("vec", ("b_z", "b_r", "b")[gate]), None, ALU.add).then_inc(gb_ready, 1)
            for gate, (name, f) in enumerate((("U_z", 0.5), ("U_r", 0.5), ("U", 0.25), ("U_r", -0.25))):
                dve.tensor_scalar(u_half[:, gate, :], part("rec", name), f, None, ALU.mult).then_inc(u_ready, 1)
            dve.wait_ge(dve_setup, 3)
            dve.tensor_copy(cond_rep[:, :, :], bcast(part("vec", "cond"), 2, [P, B, TC])).then_inc(cr_ready, 1)
            dve.wait_ge(cr_ready, 1)
            dve.tensor_copy(mask_bf[:, :], part("cst", "mask")).then_inc(u_ready, 1)
            dve.tensor_copy(ident_bf[:, :], ident).then_inc(dve_setup, 1)
            dve.tensor_tensor(sm[:, 0:HD], part("vec", "qn"), part("vec", "kn"), ALU.mult).then_inc(dve_setup, 1)
            dve.wait_ge(dve_setup, 5)
            dve.tensor_scalar(sm[:, 8:16], sm[:, 0:HD], HD ** -0.5, None, ALU.mult).then_inc(dve_setup, 1)
            dve.wait_ge(dve_setup, 6)
            dve.tensor_copy(qk_scale[:, :].rearrange("p (h d) -> p h d", d=HD), bcast(sm[:, 8:16], 1, [P, HEADS, HD])).then_inc(dve_setup, 1)

            def one_pass(c, R, before, nk):
                if nk:
                    gru(pacer(part1(c - 1, before), part2(c - 2, nk)), c, R, before)
                else:
                    gru(pacer(part1(0, before, alone=True) if before else setup()), c, R, before)
            chunks(dve, "dve", one_pass)
            begin(dve, "dve", parts_go, NC)
            merge(part1(NC - 1, R[1]), part2(NC - 2, NC))
            dve.drain().then_inc(S["parts_done"], 1)
            begin(dve, "dve", parts_go, NC + 1)
            merge(part2(NC - 1, NC))

        @block.gpsimd
        def _(pool):
            def heads_of_q():
                for h in range(0, HEADS, HG):
                    ins = pool.tensor_tensor(q_m[:, :, h:h + HG, :], bcast(q_f[:, :, :], 2, [P, B, HG, TC]),
                                             part("cst", "head_f", h, HG).unsqueeze(1).unsqueeze(3)
                                             .to_broadcast([P, B, HG, TC]), ALU.mult)
                ins.then_inc(S["qm_ready"], 1)

            def sigmoid_e():
                pool.wait_ge(S["nl_ready"], 1)
                pool.tensor_tensor(sm[:, 8:16], e_const[:, :], sm[:, 0:8], ALU.pow).then_inc(S["sig_e"], 1)

            def part1():
                pool.wait_ge(S["ms_ready"], 1)
                pool.tensor_tensor(rs[:, 2:3], rs[:, 1:2], neg_half[:, 0:1], ALU.pow).then_inc(S["r1_ready"], 1)
                pool.wait_ge(S["ssh_ready"], 1)
                pool.tensor_tensor(r_h[:, :], ss_h[:, :], neg_half[:, :], ALU.pow).then_inc(S["rh_ready"], 1)

            def part2():
                pool.wait_ge(S["ms2_ready"], 1)
                pool.tensor_tensor(rs2[:, 5:6], rs2[:, 4:5], neg_half[:, 0:1], ALU.pow).then_inc(S["r2_ready"], 1)
                pool.wait_ge(S["ge_e"], 1)
                pool.tensor_tensor(sm2[:, 32:32 + E2], e_const[:, 0:E2], sm2[:, 24:24 + E2],
                                   ALU.pow).then_inc(S["e_ready"], 1)

            def next_parts():
                pool.wait_ge(S["parts_done"], 4)
                pool.sem_clear(span(S))
                pool.drain().then_inc(parts_go, 1)

            def clear(before):
                pool.wait_ge(before["left"], 3)
                pool.sem_clear(span(before))
                pool.drain().then_inc(cleared, 1)

            pool.memset(e_const[:, :], 2.718281828459045)
            pool.memset(neg_half[:, :], -0.5)
            pool.memset(v_c[:, :], 0.0)
            pool.memset(k_c[:, :], 0.0).then_inc(pool_setup, 1)
            pool.wait_ge(pool_setup, 1)
            next_parts()
            clear(R[0])
            sigmoid_e()
            part1()
            next_parts()
            with pool.Fori(2, NC - 1, 2):
                for k in range(2):
                    clear(R[1 - k])
                    sigmoid_e()
                    heads_of_q()
                    part1()
                    part2()
                    next_parts()
            heads_of_q()
            sigmoid_e()
            part1()
            part2()
            next_parts()
            heads_of_q()
            part2()

        @block.sync
        def _(sp):
            sp.dma_start(packs["rec"][0][:, :], rec[:, :]).then_inc(in_rec, 16)
            sp.dma_start(packs["vec"][0][:, :], vec[:, :]).then_inc(in_rec, 16)
            sp.dma_start(packs["cst"][0][:, :], cst[:, :]).then_inc(in_rec, 16)
            sp.dma_start(x_sb[:, 0:NC * P], xT[:, :]).then_inc(in_x, 16)
            sp.dma_start(packs["mix"][0][:, :], mix[:, :]).then_inc(in_mix, 16)
            sp.dma_start(packs["ffn"][0][:, :], ffn[:, :]).then_inc(in_ffn, 16)
            sp.wait_ge(in_mix, 16)
            sp.wait_ge(in_ffn, 16)
            sp.sem_inc(S["parts_done"], 1)
            begin(sp, "sp", parts_go, 1)
            sp.sem_inc(S["parts_done"], 1)

            def store(tile):
                sp.sem_inc(S["fin_free"], 1)
                sp.wait_ge(S["moe_ready"], E2)
                sp.dma_start(out[bass.ds(tile, 1), :, :].rearrange("a p f -> (a p) f"), fin[:, :]).then_inc(out_done, 16)

            begin(sp, "sp", parts_go, 2)
            store(0)
            sp.sem_inc(S["parts_done"], 1)
            with sp.Fori(3, NC + 1) as c:
                begin(sp, "sp", parts_go, c)
                sp.wait_ge(out_done, 16 * (c - 2))
                store(c - 2)
                sp.sem_inc(S["parts_done"], 1)
            begin(sp, "sp", parts_go, NC + 1)
            sp.wait_ge(out_done, 16 * (NC - 1))
            store(NC - 1)
            sp.wait_ge(out_done, 16 * NC)


def constants():
    import numpy as np
    p = np.arange(P)[:, None]
    t = np.arange(TC)[None, :]
    inv = np.broadcast_to(0.5 / (np.arange(T) + 1.0), (P, T))
    mask = np.where(np.arange((2 * NC - 1) * TC)[None, :] - (NC - 1) * TC <= p % TC, 0.0, NEG)
    made = {"ident": np.eye(P), "inv": inv, "head_f": p // HD == np.arange(HEADS)[None, :],
            "head_p": p // TC == np.arange(HG)[None, :], "pick_t": p % TC == t,
            "count8": np.broadcast_to(np.arange(8), (P, 8)), "mask": mask}
    return np.concatenate([np.asarray(made[n], np.float32).reshape(P, w) for n, w in CST], axis=1)


def kernel(**inputs):
    import numpy as np
    import concourse.bacc as bacc
    from concourse import mybir as mb
    from concourse.bass_utils import run_bass_kernel_spmd as run_spmd

    a = {n: np.asarray(v) for n, v in inputs.items()}

    def rows(w):
        return np.concatenate(np.split(w, w.shape[0] // P, axis=0), axis=1)

    def square(w):
        return np.concatenate([w[k * P:(k + 1) * P, j * P:(j + 1) * P] for j in range(2) for k in range(2)], axis=1)

    col = lambda v: v.reshape(P, 1)
    wide = lambda v: np.broadcast_to(v, (P, v.shape[0]))
    c, m, f = "L0_cond_", "L0_cond2_", "L0_ffn_"
    rec = [a[c + n] for n, _ in REC]
    vec = [col(a[c + "b_z"]), col(a[c + "b_r"]), col(a[c + "b"]), col(a[f + "n1_w"]), col(a[f + "n2_w"]),
           a["cond_1024"].T, wide(a[m + "router_bias"]), wide(a[f + "qn_w"]), wide(a[f + "kn_w"])]
    mix = [a[m + "router_W"][:P], a[m + "router_W"][P:], a[m + "w1"], a[m + "w3"], rows(a[m + "w2"]),
           *a[m + "W1e"], *a[m + "W2e"]]
    ffn = [a[f + "wq"].T, a[f + "wk"].T, a[f + "wv"].T, a[f + "wo"].T,
           a[f + "gate_w"].T, a[f + "e0_up"].T, a[f + "e1_w1"].T, a[f + "e1_w2"].T, a[f + "e2_l1"].T, a[f + "e3_down"].T,
           rows(a[f + "e0_down"].T), rows(a[f + "e1_down"].T), square(a[f + "e2_l2"].T), square(a[f + "e2_l3"].T),
           rows(a[f + "e2_l4"].T), a[f + "e3_up"].T, rows(a[f + "e3_out"].T)]
    x = a["x"].reshape(B, NC, TC, D).transpose(3, 1, 0, 2).reshape(D, NC * P)
    arrays = {"xT": x, "rec": np.concatenate(rec, 1), "vec": np.concatenate(vec, 1), "cst": constants(),
              "mix": np.concatenate(mix, 1), "ffn": np.concatenate(ffn, 1)}
    arrays = {n: np.ascontiguousarray(v) for n, v in arrays.items()}

    nc = bacc.Bacc("TRN2", target_bir_lowering=False, num_devices=1)
    aps = [nc.dram_tensor(n, v.shape, mb.dt.float32, kind="ExternalInput").ap() for n, v in arrays.items()]
    out = nc.dram_tensor("out", (NC, P, D), mb.dt.float32, kind="ExternalOutput").ap()
    build(nc, *aps, out)
    got = run_spmd(nc, [arrays], core_ids=[0]).results[0]["out"]
    return got.reshape(NC, B, TC, D).transpose(1, 0, 2, 3).reshape(B, T, D)
```

```python
from contextlib import ExitStack

import concourse.bass as bass
from concourse import mybir

F32 = mybir.dt.float32
BF16 = mybir.dt.bfloat16
U32 = mybir.dt.uint32
ALU = mybir.AluOpType
ACT = mybir.ActivationFunctionType
X = mybir.AxisListType.X

P = 128
B, T, D = 4, 256, 128
TC = P // B
NC = T // TC
E1, E2 = 8, 4
HEADS, HD = 16, 8
G = 4
HG = HEADS // G
M_ZERO = 32
EPS = 1.1920929e-07
NEG = -1e30
FLT_MAX = 3.4028234663852886e38

REC = [("W_z", P), ("W_r", P), ("W", P), ("U_z", P), ("U_r", P), ("U", P), ("C_z", P), ("C_r", P), ("C", P)]
VEC = [("b_z", 1), ("b_r", 1), ("b", 1), ("n1", 1), ("n2", 1), ("cond", B), ("rbias", E1), ("qn", HD), ("kn", HD)]
CST = [("ident", P), ("inv", NC * TC), ("head_f", HEADS), ("head_p", HG), ("pick_t", TC), ("count8", 8),
       ("mask", (2 * NC - 1) * TC)]
MIX = [("rw_x", E1), ("rw_c", E1), ("w1", 2 * P), ("w3", 2 * P), ("w2", 2 * P), ("up", E1 * P), ("down", E1 * P)]
FFN = [("wq", P), ("wk", P), ("wv", P), ("wo", P),
       ("gate", E2), ("e0_up", 2 * P), ("e1_w1", 2 * P), ("e1_w2", 2 * P), ("l1", 2 * P), ("e3_down", P),
       ("e0_down", 2 * P), ("e1_down", 2 * P), ("l2", 4 * P), ("l3", 4 * P), ("l4", 2 * P),
       ("e3_up", 2 * P), ("e3_out", 2 * P)]


def columns(table):
    at, found = 0, {}
    for name, width in table:
        found[name] = (at, at + width)
        at += width
    return found, at


def build(nc, xT, rec, vec, cst, mix, ffn, out):
    with ExitStack() as ctx:
        def sb(name, *shape, dt=F32):
            return ctx.enter_context(nc.sbuf_tensor(name, [P, *shape], dt))

        def bank(name):
            return ctx.enter_context(nc.psum_tensor(name, [P, 512], F32))

        def sem(name):
            return ctx.enter_context(nc.semaphore(name))

        x_sb = sb("x_sb", (NC + 1) * P)
        packs = {}
        for name, table in (("rec", REC), ("vec", VEC), ("cst", CST), ("mix", MIX), ("ffn", FFN)):
            found, width = columns(table)
            packs[name] = (sb(name + "_sb", width), found)

        def part(pack, name, lo=0, n=None):
            t, found = packs[pack]
            a, b = found[name]
            return t[:, a + lo:(b if n is None else a + lo + n)]

        ident = part("cst", "ident")
        u_half = sb("u_half", 4, P)
        gate_bias = sb("gate_bias", 3, B)
        cond_rep = sb("cond_rep", B, TC)
        route_c = sb("route_c", E1)
        qk_scale = sb("qk_scale", P)
        mask_bf = sb("mask_bf", (2 * NC - 1) * TC, dt=BF16)
        ident_bf = sb("ident_bf", P, dt=BF16)
        e_const = sb("e_const", 8)
        neg_half = sb("neg_half", 2 * HEADS)

        h2 = sb("h2", 2, B)
        tz, tr, th = sb("tz", 2, B), sb("tr", 2, B), sb("th", 2, B)
        g_in, kept, new = sb("g_in", 2, B), sb("kept", 2, B), sb("new", 2, B)
        idle = sb("idle", 384, dt=BF16)
        run = sb("run", B, TC)

        mean = sb("mean", B, TC)
        x1 = sb("x1", P)
        x1t = sb("x1t", P)
        sm = sb("sm", 64)
        ix1, ix2 = sb("ix1", 8, dt=U32), sb("ix2", 8, dt=U32)
        comb = sb("comb", E1)
        th_sh, s_a, s_h = sb("th_sh", 2, P), sb("s_a", 2, P), sb("s_h", 2, P)
        ge = sb("ge", E1, P)
        acc = sb("acc", P)
        x2 = sb("x2", P)
        sq = sb("sq", 2 * P)
        rs = sb("rs", 8)
        hn, hn_f = sb("hn", P), sb("hn_f", P)
        ss_h, r_h = sb("ss_h", 2 * HEADS), sb("r_h", 2 * HEADS)
        q_n, q_s, k_n = sb("q_n", P), sb("q_s", P), sb("k_n", P)
        v_n, k_f, q_f = sb("v_n", P), sb("k_f", P), sb("q_f", B, TC)
        q_m = sb("q_m", B, HEADS, TC)
        k_c = sb("k_c", NC * P)
        v_c = sb("v_c", NC * G * P)
        nmax, psum_r = sb("nmax", 16), sb("psum_r", 16)
        p_e = sb("p_e", 2, NC * P)
        p_t = sb("p_t", 2, NC * P)
        inv_sum = sb("inv_sum", 16)
        ao_m = sb("ao_m", B, G, 32)
        ao_f = sb("ao_f", P)
        xn, xn_f = sb("xn", P), sb("xn_f", P)
        x3 = sb("x3", P)
        sm2 = sb("sm2", 96)
        sq2 = sb("sq2", P)
        rs2 = sb("rs2", 8)
        wts = sb("wts", 8)
        gf = sb("gf", 11, P)
        th_e, e_a, e_h = sb("th_e", 2, P), sb("e_a", 2, P), sb("e_h", 2, P)
        base = sb("base", P)
        fin = sb("fin", P)

        bk_r, bk_z, bk_h = bank("bk_r"), bank("bk_z"), bank("bk_h")
        b0, b1, b2, b3, b4 = (bank(f"b{i}") for i in range(5))

        in_rec, in_x, in_mix, in_ffn = sem("in_rec"), sem("in_x"), sem("in_mix"), sem("in_ffn")
        u_ready, rec_ps, gb_ready, cr_ready = sem("u_ready"), sem("rec_ps"), sem("gb_ready"), sem("cr_ready")
        rc_ps, dve_setup, pool_setup = sem("rc_ps"), sem("dve_setup"), sem("pool_setup")
        idle_ready = sem("idle_ready")
        parts_go, out_done = sem("parts_go"), sem("out_done")
        begun = {n: sem("begun_" + n) for n in ("pe", "act", "dve", "sp")}

        names = """r_acc z_acc h_acc r_act z_act h_act g_ready kept_ready new_ready h_ready run_ready left""".split()
        R = [{n: sem(f"{n}_{k}") for n in names} for k in ("even", "odd")]
        cleared = sem("cleared")

        names = """mean_ready x1_ready nl_ready sig_e dchain dchain2 dchain3 e_ready comb_ready x1t_ps x1t_ready sh_ps sh_th sa_ready
            sh_ready up_ps ge_ready shd_ps dn_ps acc_ready x2_ready ms_ready r1_ready hn_ready hn_ps hnf_ready qkv_ps
            sq_ready ssh_ready rh_ready qn_ready qs_ready kn_ready qt_ps kt_ps qm_ready qf_ready kf_ready vn_ready kc_ready vc_ready
            sc_ps nmax_ready pe_ready pt_ps pt_ready pv_ps inv_ready aom_ready ao_ps aof_ready wo_ps x3_ready
            ms2_ready r2_ready xn_ready xn_ps xnf_ready gt_ps ge_nl ge_e hid_ps hid_ready e1_ps
            e1_th ea_ready eh_ready o_ps moe_ready base_ready x3c_ready fin_free parts_done""".split()
        S = {n: sem(n) for n in names}

        def span(sems):
            nums = sorted(s.num for s in sems.values())
            assert nums == list(range(nums[0], nums[0] + len(nums)))
            return range(nums[0], nums[-1] + 1)

        block = ctx.enter_context(nc.Block())

        def pacer(*programs):
            due = [next(p, None) for p in programs]

            def advance(step):
                for n, p in enumerate(programs):
                    while due[n] is not None and due[n] < step + 0.05:
                        due[n] = next(p, None)
            return advance

        def merge(*programs, after=None):
            advance = pacer(*programs)
            for t in range(2 * TC):
                advance((t + 1) / 2 - 0.25)
                advance((t + 1) / 2 - 0.05)
                if after:
                    after((t + 1) / 2)

        def earlier(program, steps):
            for step in program:
                yield step - steps

        SCORES = (b2, b1)

        LOOPS = ((2, 2 + NC // 2, NC // 2), (2 + NC // 2, NC, NC - 2))

        def begin(engine, name, go, n):
            engine.wait_ge(go, n)
            engine.sem_inc(begun[name], 1)

        def enter(engine, name, t, c):
            if t == 0 and not (isinstance(c, int) and c == 0):
                begin(engine, name, parts_go, c)

        def leave(engine, t, before):
            if t == 1 and before:
                engine.drain().then_inc(before["left"], 1)
            if t == TC - 1:
                engine.drain().then_inc(S["parts_done"], 1)

        def chunks(engine, name, one_pass):
            def both(c, k, nk):
                begin(engine, name, cleared, c - 1)
                one_pass(c, R[k], R[1 - k], nk)
            one_pass(0, R[0], None, None)
            one_pass(1, R[1], R[0], None)
            for lo, hi, nk in LOOPS:
                with engine.Fori(lo, hi - 1, 2) as c:
                    both(c, 0, nk)
                    both(c + 1, 1, nk)

        ALL = 1e9
        WINDOW, WINDOW_BOTH = 1000, 1150

        def bcast(ap, axis, shape):
            return ap.unsqueeze(axis).to_broadcast(shape)

        def tile_cols(tile):
            return bass.ds(tile * P, P)

        @block.tensor
        def _(pe):
            streamed = [0]
            window = [WINDOW]

            def keep_clock(bk):
                while streamed[0] < window[0]:
                    n = min(3 * P, window[0] - streamed[0])
                    mm(bk[:, P:P + n], idle[:, 0:P], idle[:, 0:n], start=False)
                streamed[0] = 0

            def table_load():
                streamed[0] -= 2200

            def mm(o, w, r, start=True, stop=True):
                streamed[0] += o.free_size() * w.shape[0] * (4 if w.dtype == F32 else 1) // P
                return pe.matmul(o, w, r, start=start, stop=stop, skip_group_check=True)

            def transpose(o, x):
                streamed[0] += P
                return pe.transpose(o, x, ident)

            def fill(gate, bk, chunk):
                mm(bk[:, 0:P], part("rec", ("W_z", "W_r", "W")[gate]), x_sb[:, tile_cols(chunk)])
                return mm(bk[:, 0:P], ident, bcast(gate_bias[:, gate, :], 2, [P, B, TC]), start=False)

            def at(bk, t):
                return bk[:, t:P:TC]

            def gru(advance, c, R, before):
                streamed[0] = 0
                for t in range(TC):
                    if t == 0 and not before:
                        mm(at(bk_r, t), u_half[:, 1, :], h2[:, 0, :], start=False).then_inc(R["r_acc"], 1)
                    else:
                        last, n = (R, t) if t else (before, TC)
                        pe.wait_ge(last["kept_ready"], n)
                        mm(at(bk_r, t), u_half[:, 3, :], kept[:, t % 2, :], start=False)
                        advance(t - 0.4)
                        keep_clock(bk_r)
                        pe.wait_ge(last["new_ready"], n)
                        mm(at(bk_r, t), u_half[:, 1, :], new[:, t % 2, :], start=False).then_inc(R["r_acc"], 1)
                        pe.wait_ge(last["h_ready"], n)
                    mm(at(bk_z, t), u_half[:, 0, :], h2[:, t % 2, :], start=False).then_inc(R["z_acc"], 1)
                    if t == 0:
                        if before:
                            pe.wait_ge(before["h_act"], TC)
                        fill(2, bk_h, c)
                    enter(pe, "pe", t, c)
                    advance(t + 0.1 if t < TC - 1 else ALL)
                    leave(pe, t, before)
                    keep_clock(bk_h)
                    pe.wait_ge(R["g_ready"], t + 1)
                    mm(at(bk_h, t), u_half[:, 2, :], g_in[:, t % 2, :], start=False).then_inc(R["h_acc"], 1)
                pe.wait_ge(R["r_act"], TC)
                fill(1, bk_r, c + 1)
                pe.wait_ge(R["z_act"], TC)
                fill(0, bk_z, c + 1)

            def setup():
                yield 20.1
                pe.wait_ge(in_mix, 16)
                pe.wait_ge(cr_ready, 1)
                mm(b1[:, 0:E1], cond_rep[:, :, :], part("mix", "rw_c")).then_inc(rc_ps, 1)

            def part1(i):
                yield 0.6
                pe.wait_ge(S["x1_ready"], 1)
                mm(b0[:, 0:E1], x1[:, :], part("mix", "rw_x"))
                transpose(b0[:, P:2 * P], x1[:, :]).then_inc(S["x1t_ps"], 1)
                for e in range(E1):
                    yield 1.6 + e / 2
                    if e == 0:
                        pe.wait_ge(S["nl_ready"], 1)
                        pe.wait_ge(S["x1t_ready"], 1)
                    else:
                        pe.wait_ge(S["ge_ready"], e)
                    mm(b0[:, 0:P], part("mix", "up", e * P, P), x1[:, :]).then_inc(S["up_ps"], 1)
                for j in range(2):
                    yield (5.6, 7.1)[j]
                    pe.wait_ge(S[("ge_ready", "sh_ready")[j]], (E1, 1)[j])
                    mm(b0[:, 0:P], part("mix", "w1", j * P, P), x1[:, :])
                    mm(b0[:, P:2 * P], part("mix", "w3", j * P, P), x1[:, :]).then_inc(S["sh_ps"], 1)
                yield 8.1
                pe.wait_ge(S["sh_ready"], 2)
                mm(b0[:, 0:P], s_h[:, 0, :], part("mix", "w2", 0, P), stop=False)
                mm(b0[:, 0:P], s_h[:, 1, :], part("mix", "w2", P, P), start=False).then_inc(S["shd_ps"], 1)
                for e in range(E1):
                    yield 8.6 + e / 2
                    pe.wait_ge(S["acc_ready"], e + 1)
                    mm(b0[:, 0:P], ge[:, e, :], part("mix", "down", e * P, P)).then_inc(S["dn_ps"], 1)
                yield 14.6
                pe.wait_ge(S["hn_ready"], 1)
                transpose(b0[:, 0:P], hn[:, :]).then_inc(S["hn_ps"], 1)
                yield 15.1
                pe.wait_ge(S["hnf_ready"], 1)
                mm(b0[:, 0:P], hn_f[:, :], part("ffn", "wv"))
                mm(b0[:, P:2 * P], hn_f[:, :], part("ffn", "wq"))
                mm(b0[:, 2 * P:3 * P], hn_f[:, :], part("ffn", "wk")).then_inc(S["qkv_ps"], 1)
                yield 20.6
                pe.wait_ge(S["vn_ready"], 1)
                pe.wait_ge(S["kn_ready"], 1)
                pe.wait_ge(S["qn_ready"], 1)
                transpose(b0[:, 0:P], k_n[:, :]).then_inc(S["kt_ps"], 1)
                yield 21.1
                pe.wait_ge(S["qs_ready"], 1)
                pe.wait_ge(S["kf_ready"], 1)
                transpose(b0[:, P:2 * P], q_s[:, :]).then_inc(S["qt_ps"], 1)

            def attention(i, nk, banks=SCORES):
                keys = nk * TC
                ao = b4[:, :].rearrange("p (b g f) -> p b g f", b=B, g=G)
                rounds = (nk + 3) // 4

                def scores(m):
                    if m == 0:
                        pe.wait_ge(S["kc_ready"], 1)
                    if m % 2 == 0:
                        pe.wait_ge(S["qm_ready"], m // 2 + 1)
                    if m >= len(banks):
                        pe.wait_ge(S["pe_ready"], 2 * (m - len(banks) + 1))
                    bk = banks[m % len(banks)]
                    for n in (2 * m, 2 * m + 1):
                        g, b = n // B, n % B
                        cols = slice((n % 2) * keys, (n % 2 + 1) * keys)
                        mm(bk[:, cols], q_m[:, b, g * HG:(g + 1) * HG, :],
                           k_c[:, :].rearrange("p (i b t) -> p i b t", b=B, t=TC)[:, 0:nk, b, :], stop=False)
                        last = mm(bk[:, cols], ident_bf[:, :], mask_bf[:, bass.ds((NC - 1 - i) * TC, keys)], start=False)
                    last.then_inc(S["sc_ps"], 1)

                def turn(g, n):
                    pe.wait_ge(S["pe_ready"], B * (g + 1))
                    if g or n:
                        pe.wait_ge(S["pt_ready"], g * (nk // 2) + 2 * n)
                    for c in range(4 * n, min(4 * n + 4, nk)):
                        last = transpose(b3[:, (c % 4) * P:(c % 4 + 1) * P], p_e[:, g % 2, c * P:(c + 1) * P])
                    last.then_inc(S["pt_ps"], 1)

                def values(g, c):
                    if g == 0 and c == 0:
                        pe.wait_ge(S["vc_ready"], B)
                    pe.wait_ge(S["pt_ready"], g * (nk // 2) + c // 2 + 1)
                    last = mm(ao[:, :, g, :], p_t[:, g % 2, c * P:(c + 1) * P],
                              v_c[:, (c * G + g) * P:(c * G + g + 1) * P], start=(c == 0), stop=(c == nk - 1))
                    if c == nk - 1:
                        last.then_inc(S["pv_ps"], 1)

                pieces = [(6.1, table_load, ())]
                for g in range(G):
                    at = 4.6 + 3 * g
                    pieces += [(at, scores, (2 * g,)), (at + 1.0, scores, (2 * g + 1,))]
                    pieces += [(at + (3.5, 4.5, 5.0, 5.5)[c // 2], values, (g, c)) for c in range(nk)]
                    pieces += [(at + (2.5, 4.5)[n], turn, (g, n)) for n in range(rounds)]
                for at, piece, args in sorted(pieces, key=lambda p: p[0]):
                    yield at
                    piece(*args)
                yield 21.1
                pe.wait_ge(S["aom_ready"], HG)
                for b in range(B):
                    last = mm(b2[:, b * TC:(b + 1) * TC], ao_m[:, b, :, :], part("cst", "pick_t"))
                last.then_inc(S["ao_ps"], 1)
                yield 21.6
                pe.wait_ge(S["aof_ready"], 1)
                mm(b3[:, 0:P], ao_f[:, :], part("ffn", "wo")).then_inc(S["wo_ps"], 1)

            def mixture(banks=(b2, b3, b4), apart=False):
                ba, bb, bc = banks
                yield 23.6
                if not apart:
                    pe.wait_ge(S["xn_ready"], 1)
                transpose(ba[:, 0:P], xn[:, :]).then_inc(S["xn_ps"], 1)
                yield 24.1
                pe.wait_ge(S["xnf_ready"], 1)
                mm(bc[:, 0:E2], xn_f[:, :], part("ffn", "gate")).then_inc(S["gt_ps"], 1)

                def f(name, k=0):
                    return part("ffn", name, k * P, P)

                def hidden(n, pieces):
                    if n >= 2:
                        pe.wait_ge(S["hid_ready"], n - 1)
                    for k, (w, x) in enumerate(pieces):
                        last = mm((ba, bb)[n % 2][:, 0:P], w, x, start=(k == 0), stop=(k == len(pieces) - 1))
                    last.then_inc(S["hid_ps"], 1)

                def gated(j):
                    mm(bc[:, 0:P], f("e1_w1", j), xn_f[:, :])
                    mm(bc[:, P:2 * P], f("e1_w2", j), xn_f[:, :]).then_inc(S["e1_ps"], 1)

                def result(bk, name, h):
                    mm(bk[:, 0:P], h[0], f(name, 0), stop=False)
                    mm(bk[:, 0:P], h[1], f(name, 1), start=False).then_inc(S["o_ps"], 1)

                hidden(0, [(f("e0_up", 0), xn_f[:, :])])
                yield 24.6
                table_load()
                hidden(1, [(f("e0_up", 1), xn_f[:, :])])
                hidden(2, [(f("l1", 0), xn_f[:, :])])
                yield 25.1
                hidden(3, [(f("l1", 1), xn_f[:, :])])
                pe.wait_ge(S["ge_nl"], 1)
                gated(0)
                yield 25.6
                hidden(4, [(f("e3_down"), xn_f[:, :])])
                yield 26.1
                pe.wait_ge(S["hid_ready"], 4)
                hidden(5, [(f("l2", 0), gf[:, 2, :]), (f("l2", 1), gf[:, 3, :])])
                pe.wait_ge(S["eh_ready"], 1)
                gated(1)
                yield 26.6
                hidden(6, [(f("l2", 2), gf[:, 2, :]), (f("l2", 3), gf[:, 3, :])])
                yield 27.1
                hidden(7, [(f("e3_up", 0), gf[:, 4, :])])
                hidden(8, [(f("e3_up", 1), gf[:, 4, :])])
                yield 27.6
                pe.wait_ge(S["hid_ready"], 7)
                hidden(9, [(f("l3", 0), gf[:, 5, :]), (f("l3", 1), gf[:, 6, :])])
                pe.wait_ge(S["eh_ready"], 2)
                result(bc, "e0_down", (gf[:, 0, :], gf[:, 1, :]))
                yield 28.1
                hidden(10, [(f("l3", 2), gf[:, 5, :]), (f("l3", 3), gf[:, 6, :])])
                yield 28.6
                pe.wait_ge(S["hid_ready"], 10)
                result(bb, "e1_down", (e_h[:, 0, :], e_h[:, 1, :]))
                yield 29.1
                pe.wait_ge(S["hid_ready"], 11)
                result(ba, "e3_out", (gf[:, 7, :], gf[:, 8, :]))
                yield 29.6
                pe.wait_ge(S["moe_ready"], 1)
                result(bc, "l4", (gf[:, 9, :], gf[:, 10, :]))

            pe.wait_ge(idle_ready, 1)
            for _ in range(40):
                mm(bk_r[:, 0:3 * P], idle[:, 0:P], idle[:, :])
            pe.wait_ge(in_rec, 3 * 16)
            for gate in range(3):
                last = mm(b0[:, gate * B:(gate + 1) * B], part("rec", ("C_z", "C_r", "C")[gate]), part("vec", "cond"))
            last.then_inc(rec_ps, 1)
            pe.wait_ge(in_x, 16)
            pe.wait_ge(gb_ready, 3)
            fill(0, bk_z, 0)
            fill(1, bk_r, 0)
            pe.wait_ge(u_ready, 5)

            def one_pass(c, R, before, nk):
                if nk:
                    window[0] = WINDOW_BOTH
                    gru(pacer(part1(c - 1), attention(c - 2, nk), mixture()), c, R, before)
                else:
                    gru(pacer(part1(0) if before else setup()), c, R, before)
            chunks(pe, "pe", one_pass)

            def busy(*levels):
                def after(step):
                    window[0] = [n for start, n in levels if step > start][-1]
                    keep_clock(bk_h)
                return after

            begin(pe, "pe", parts_go, NC)
            merge(part1(NC - 1), attention(NC - 2, NC), after=busy((0, 0), (0.6, 1000), (5.5, 0)))
            pe.drain().then_inc(S["parts_done"], 1)
            streamed[0] = -1000
            keep_clock(bk_h)
            begin(pe, "pe", parts_go, NC + 1)
            merge(earlier(mixture((b0, bk_z, bk_r), apart=True), 23), attention(NC - 1, NC), after=busy((0, 900), (6, 0)))
            pe.drain().then_inc(S["parts_done"], 1)
            begin(pe, "pe", parts_go, NC + 2)
            merge(earlier(mixture(apart=True), 23), after=busy((0, 0)))

        @block.scalar
        def _(act):
            def at(bk, t):
                return bk[:, t:P:TC]

            def gru(advance, c, R, before):
                for t in range(TC):
                    act.wait_ge(R["r_acc"], t + 1)
                    act.activation(tr[:, t % 2, :], at(bk_r, t), ACT.Tanh, scale=0.5).then_inc(R["r_act"], 1)
                    act.wait_ge(R["z_acc"], t + 1)
                    act.activation(tz[:, t % 2, :], at(bk_z, t), ACT.Tanh, scale=0.5).then_inc(R["z_act"], 1)
                    enter(act, "act", t, c)
                    advance(t + 0.3 if t < TC - 1 else ALL)
                    leave(act, t, before)
                    act.wait_ge(R["h_acc"], t + 1)
                    act.activation(th[:, t % 2, :], at(bk_h, t), ACT.Tanh).then_inc(R["h_act"], 1)
                    if t < TC - 1:
                        advance(t + 0.7)

            def part1(i):
                yield 1.3
                act.wait_ge(S["base_ready"], 1)
                act.wait_ge(S["nl_ready"], 1)
                act.wait_ge(S["x1t_ps"], 1)
                act.copy(x1t[:, :], b0[:, P:2 * P]).then_inc(S["x1t_ready"], 1)
                for e in range(E1):
                    yield 1.7 + (e + 1) // 2 - 0.4 * (e % 2)
                    act.wait_ge(S["up_ps"], e + 1)
                    act.activation(ge[:, e, :], b0[:, 0:P], ACT.Gelu).then_inc(S["ge_ready"], 1)
                for j in range(2):
                    yield 6.3 + j
                    act.wait_ge(S["sh_ps"], j + 1)
                    act.activation(th_sh[:, j, :], b0[:, 0:P], ACT.Tanh, scale=0.5).then_inc(S["sh_th"], 1)
                yield 14.7
                act.wait_ge(S["hn_ps"], 1)
                act.copy(hn_f[:, :], b0[:, 0:P]).then_inc(S["hnf_ready"], 1)
                yield 15.7
                act.wait_ge(S["qkv_ps"], 1)
                act.activation(sq[:, :], b0[:, P:3 * P], ACT.Square).then_inc(S["sq_ready"], 1)
                yield 16.3
                act.wait_ge(S["qkv_ps"], 1)
                act.copy(v_n[:, :], b0[:, 0:P]).then_inc(S["vn_ready"], 1)
                yield 20.7
                act.wait_ge(S["kt_ps"], 1)
                act.copy(k_f[:, :], b0[:, 0:P]).then_inc(S["kf_ready"], 1)
                yield 21.3
                act.wait_ge(S["qt_ps"], 1)
                act.copy(q_f[:, :, :], b0[:, P:2 * P].rearrange("p (b t) -> p b t", b=B)).then_inc(S["qf_ready"], 1)

            def attention(i, nk, banks=SCORES):
                keys = nk * TC
                rounds = (nk + 3) // 4
                yield 0.7
                act.copy(k_c[:, tile_cols(i)], k_f[:, :]).then_inc(S["kc_ready"], 1)

                def cache_v(b):
                    rows = slice(TC * b, TC * (b + 1))
                    act.copy(v_c[rows, bass.ds(i * (G * P), G * P)].rearrange("p (g b f) -> p g b f", g=G, b=B)[:, :, b, :],
                             v_n[rows, :].rearrange("p (g f) -> p g f", g=G)).then_inc(S["vc_ready"], 1)

                def exps(n):
                    g, b = n // B, n % B
                    act.wait_ge(S["nmax_ready"], n // 2 + 1)
                    if b == 0 and g >= 2:
                        act.wait_ge(S["pt_ps"], (g - 1) * rounds)
                    o = p_e[:, g % 2, :].rearrange("p (c b t) -> p c b t", b=B, t=TC)[:, 0:nk, b, :]
                    cols = slice((n % 2) * keys, (n % 2 + 1) * keys)
                    act.activation(o, banks[n // 2 % len(banks)][:, cols].rearrange("p (c t) -> p c t", t=TC), ACT.Exp,
                                   bias=nmax[:, n:n + 1],
                                   accum_out=psum_r[:, b * G + g:b * G + g + 1]).then_inc(S["pe_ready"], 1)

                def spread(g, n, m):
                    act.wait_ge(S["pt_ps"], g * rounds + n + 1)
                    if g >= 2 and n == 0 and m == 0:
                        act.wait_ge(S["pv_ps"], g - 1)
                    if 4 * n + 2 * m < nk:
                        lo = n * 512 + m * 256
                        act.copy(p_t[:, g % 2, lo:lo + 256], b3[:, m * 256:m * 256 + 256]).then_inc(S["pt_ready"], 1)

                pieces = [(1.7 + b, cache_v, (b,)) for b in range(B)]
                for g in range(G):
                    at = 5.7 + 3 * g
                    pieces += [(at + k // 2, exps, (4 * g + k,)) for k in range(4)]
                    pieces += [(at + (2.0, 2.0, 3.6, 4.0)[m], spread, (g, m // 2, m % 2)) for m in range(2 * rounds)]
                for at, piece, args in sorted(pieces, key=lambda p: p[0]):
                    yield at
                    piece(*args)
                yield 21.3
                act.wait_ge(S["ao_ps"], 1)
                act.copy(ao_f[:, :], b2[:, 0:P]).then_inc(S["aof_ready"], 1)

            def mixture(banks=(b2, b3, b4), apart=False):
                ba, bb, bc = banks
                yield 23.7
                act.wait_ge(S["xn_ps"], 1)
                act.copy(xn_f[:, :], ba[:, 0:P]).then_inc(S["xnf_ready"], 1)

                def gelu(n):
                    act.wait_ge(S["hid_ps"], n + 1)
                    act.activation(gf[:, n, :], (ba, bb)[n % 2][:, 0:P], ACT.Gelu).then_inc(S["hid_ready"], 1)

                def tanh(j):
                    act.wait_ge(S["e1_ps"], j + 1)
                    act.activation(th_e[:, j, :], bc[:, 0:P], ACT.Tanh, scale=0.5).then_inc(S["e1_th"], 1)

                yield 24.3
                gelu(0)
                yield 24.7
                gelu(1)
                gelu(2)
                yield 25.3
                gelu(3)
                tanh(0)
                yield 25.7
                gelu(4)
                yield 26.3
                gelu(5)
                tanh(1)
                yield 26.7
                gelu(6)
                yield 27.3
                gelu(7)
                gelu(8)
                yield 27.7
                gelu(9)
                yield 28.3
                gelu(10)

            act.preload_act_table(ACT.Gelu)

            def one_pass(c, R, before, nk):
                if nk:
                    gru(pacer(part1(c - 1), attention(c - 2, nk), mixture()), c, R, before)
                else:
                    gru(pacer(part1(0)) if before else pacer(), c, R, before)
            chunks(act, "act", one_pass)
            begin(act, "act", parts_go, NC)
            merge(part1(NC - 1), attention(NC - 2, NC))
            act.drain().then_inc(S["parts_done"], 1)
            begin(act, "act", parts_go, NC + 1)
            merge(earlier(mixture((b0, bk_z, bk_r), apart=True), 23), attention(NC - 1, NC))
            act.drain().then_inc(S["parts_done"], 1)
            begin(act, "act", parts_go, NC + 2)
            merge(earlier(mixture(apart=True), 23))

        @block.vector
        def _(dve):
            def gru(advance, c, R, before):
                def add_run(t):
                    dve.wait_ge(R["h_ready"], t + 1)
                    if t >= 1:
                        dve.wait_ge(R["run_ready"], t)
                    prev = (t - 1) % TC
                    dve.tensor_tensor(run[:, :, t], run[:, :, prev], h2[:, (t + 1) % 2, :],
                                      ALU.add).then_inc(R["run_ready"], 1)

                for t in range(TC):
                    h, nxt = h2[:, t % 2, :], (t + 1) % 2
                    dve.wait_ge(R["r_act"], t + 1)
                    if t >= 1:
                        dve.wait_ge(R["h_ready"], t)
                    elif before:
                        dve.wait_ge(before["h_ready"], TC)
                    dve.scalar_tensor_tensor(g_in[:, t % 2, :], tr[:, t % 2, :], 1.0, h, ALU.add,
                                             ALU.mult).then_inc(R["g_ready"], 1)
                    enter(dve, "dve", t, c)
                    advance(t + 0.2)
                    if t >= 1:
                        add_run(t - 1)
                    dve.wait_ge(R["z_act"], t + 1)
                    dve.scalar_tensor_tensor(kept[:, nxt, :], tz[:, t % 2, :], 1.0, h, ALU.subtract,
                                             ALU.mult).then_inc(R["kept_ready"], 1)
                    advance(t + 0.4 if t < TC - 1 else ALL)
                    leave(dve, t, before)
                    dve.wait_ge(R["h_act"], t + 1)
                    dve.scalar_tensor_tensor(new[:, nxt, :], tz[:, t % 2, :], 1.0, th[:, t % 2, :], ALU.add,
                                             ALU.mult).then_inc(R["new_ready"], 1)
                    dve.wait_ge(R["new_ready"], t + 1)
                    dve.scalar_tensor_tensor(h2[:, nxt, :], kept[:, nxt, :], -0.5, new[:, nxt, :], ALU.mult,
                                             ALU.add).then_inc(R["h_ready"], 1)
                    if t < TC - 1:
                        advance(t + 0.8)
                add_run(TC - 1)

            def chained(name):
                count = [0]

                def step(ins):
                    count[0] += 1
                    ins.then_inc(S[name], 1)

                def after():
                    dve.wait_ge(S[name], count[0])
                return step, after

            count8 = part("cst", "count8")

            def setup():
                yield 15.8
                dve.wait_ge(in_ffn, 16)
                for lo, hi, w in (("wq", "wv", "n1"), ("gate", "e3_down", "n2")):
                    t, found = packs["ffn"]
                    cols = t[:, found[lo][0]:found[hi][1]]
                    dve.tensor_scalar(cols, cols, part("vec", w), None, ALU.mult).then_inc(dve_setup, 1)
                    yield 17.8
                yield 21.4
                dve.wait_ge(rc_ps, 1)
                dve.tensor_copy(route_c[:, :], b1[:, 0:E1]).then_inc(dve_setup, 1)

            def part1(i, last_run, alone=False):
                step, after = chained("dchain")
                yield 0.2
                if alone:
                    dve.sem_inc(S["base_ready"], 1)
                dve.wait_ge(last_run["run_ready"], TC)
                inv = part("cst", "inv").rearrange("p (c t) -> p c t", t=TC)
                dve.tensor_tensor(mean[:, :, :], run[:, :, :],
                                  inv[:, bass.ds(i, 1), :].to_broadcast([P, B, TC]), ALU.mult).then_inc(S["mean_ready"], 1)
                yield 0.4
                dve.wait_ge(S["mean_ready"], 1)
                dve.tensor_tensor(x1[:, :], mean[:, :, :].rearrange("p b t -> p (b t)"), x_sb[:, tile_cols(i)],
                                  ALU.add).then_inc(S["x1_ready"], 1)
                nl, e1, s, sel, mx, first, mask, q = (sm[:, 8 * k:8 * k + 8] for k in range(8))
                yield 0.8
                dve.wait_ge(S["x1t_ps"], 1)
                dve.scalar_tensor_tensor(nl, b0[:, 0:E1], -1.0, route_c[:, :], ALU.mult,
                                         ALU.subtract).then_inc(S["nl_ready"], 1)

                def swiglu(j, bk):
                    yield 6.4 + j
                    dve.wait_ge(S["sh_th"], j + 1)
                    dve.scalar_tensor_tensor(s_a[:, j, :], th_sh[:, j, :], 1.0, bk[:, 0:P], ALU.add,
                                             ALU.mult).then_inc(S["sa_ready"], 1)
                    yield 6.8 + j
                    dve.wait_ge(S["sa_ready"], j + 1)
                    dve.tensor_tensor(s_h[:, j, :], s_a[:, j, :], bk[:, P:2 * P], ALU.mult).then_inc(S["sh_ready"], 1)

                yield 3.2
                dve.wait_ge(S["sig_e"], 1)
                step(dve.tensor_scalar(e1, e1, 1.0, None, ALU.add))
                yield 3.4
                after()
                step(dve.reciprocal(s, e1))
                yield 3.8
                after()
                step(dve.tensor_tensor(sel, s, part("vec", "rbias"), ALU.add))
                yield 4.2
                after()
                step(dve.max(mx, sel))
                yield 4.4
                after()
                step(dve.max_index(ix1[:, :], mx, sel))
                yield 4.8
                after()
                step(dve.tensor_scalar(first, count8, ix1[:, 0:1], None, ALU.is_equal))
                yield 5.2
                after()
                step(dve.scalar_tensor_tensor(mask, count8, ix1[:, 1:2], first, ALU.is_equal, ALU.add))
                yield 5.4
                after()
                den, ok = q[:, 0:1], q[:, 1:2]
                step(dve.scalar_tensor_tensor(sel, mask, 1.0, s, ALU.mult, ALU.mult, accum_out=den))
                yield 5.8
                after()
                step(dve.tensor_scalar(ok, den, 1e-9, None, ALU.is_gt))
                step(dve.tensor_scalar(q[:, 2:3], den, 1e-9, None, ALU.add))
                yield 6.2
                after()
                step(dve.reciprocal(q[:, 3:4], q[:, 2:3]))
                step(dve.tensor_scalar(q[:, 4:5], ok, -0.5, 0.5, ALU.mult, ALU.add))
                yield from swiglu(0, b0)
                after()
                step(dve.tensor_tensor(q[:, 5:6], q[:, 3:4], ok, ALU.mult))
                yield 7.2
                step(dve.tensor_scalar(first, mask, q[:, 4:5], None, ALU.mult))
                yield from swiglu(1, b0)
                after()
                dve.scalar_tensor_tensor(comb[:, :], sel, q[:, 5:6], first, ALU.mult,
                                         ALU.add).then_inc(S["comb_ready"], 1)
                yield 8.4
                dve.wait_ge(S["shd_ps"], 1)
                dve.tensor_scalar(acc[:, :], b0[:, 0:P], 0.5, None, ALU.mult).then_inc(S["acc_ready"], 1)
                dve.wait_ge(S["comb_ready"], 1)
                for e in range(E1):
                    yield 8.8 + e / 2
                    dve.wait_ge(S["dn_ps"], e + 1)
                    dve.wait_ge(S["acc_ready"], e + 1)
                    dve.scalar_tensor_tensor(acc[:, :], b0[:, 0:P], comb[:, e:e + 1], acc[:, :], ALU.mult,
                                             ALU.add).then_inc(S["acc_ready"], 1)
                yield 12.8
                dve.wait_ge(S["acc_ready"], E1 + 1)
                dve.wait_ge(S["base_ready"], 1)
                dve.tensor_scalar(x2[:, :], acc[:, :], 1.0 / 3.0, None, ALU.mult).then_inc(S["x2_ready"], 1)
                yield 13.2
                dve.wait_ge(S["x2_ready"], 1)
                step(dve.scalar_tensor_tensor(acc[:, :], x2[:, :], 1.0, x2[:, :], ALU.mult, ALU.mult,
                                              accum_out=rs[:, 0:1]))
                yield 13.4
                after()
                dve.tensor_scalar(rs[:, 1:2], rs[:, 0:1], 1.0 / D, EPS, ALU.mult, ALU.add).then_inc(S["ms_ready"], 1)
                yield 14.2
                dve.wait_ge(S["r1_ready"], 1)
                dve.tensor_scalar(hn[:, :], x2[:, :], rs[:, 2:3], None, ALU.mult).then_inc(S["hn_ready"], 1)
                yield 15.8
                dve.wait_ge(S["sq_ready"], 1)
                step(dve.tensor_reduce(ss_h[:, :], sq[:, :].rearrange("p (h d) -> p h d", d=HD), X, ALU.add))
                yield 16.2
                after()
                dve.tensor_scalar(ss_h[:, :], ss_h[:, :], 1.0 / HD, EPS, ALU.mult, ALU.add).then_inc(S["ssh_ready"], 1)

                def heads(ap):
                    return ap.rearrange("p (h d) -> p h d", d=HD)

                yield 19.8
                dve.wait_ge(S["vn_ready"], 1)
                dve.wait_ge(S["rh_ready"], 1)
                dve.tensor_tensor(heads(k_n[:, :]), heads(b0[:, 2 * P:3 * P]), bcast(r_h[:, HEADS:], 2, [P, HEADS, HD]),
                                  ALU.mult).then_inc(S["kn_ready"], 1)
                yield 20.2
                dve.tensor_tensor(heads(q_n[:, :]), heads(b0[:, P:2 * P]), bcast(r_h[:, 0:HEADS], 2, [P, HEADS, HD]),
                                  ALU.mult).then_inc(S["qn_ready"], 1)
                yield 20.8
                dve.wait_ge(S["qn_ready"], 1)
                dve.tensor_tensor(q_s[:, :], q_n[:, :], qk_scale[:, :], ALU.mult).then_inc(S["qs_ready"], 1)

            def attention(i, nk, banks=SCORES, late=False):
                step, after = chained("dchain2")
                keys = nk * TC
                def take_over(at):
                    yield at[0]
                    dve.tensor_copy(x3[:, :], x2[:, :]).then_inc(S["x3c_ready"], 1)
                    yield at[1]
                    dve.tensor_tensor(base[:, :], x2[:, :], x1t[:, :], ALU.add).then_inc(S["base_ready"], 1)

                if not late:
                    yield from take_over((0.8, 1.2))
                for m in range(2 * G):
                    yield 4.8 + 3 * (m // 2) + m % 2
                    dve.wait_ge(S["sc_ps"], m + 1)
                    dve.tensor_reduce(nmax[:, 2 * m:2 * m + 2], banks[m % len(banks)][:, 0:2 * keys].rearrange("p (n k) -> p n k", n=2),
                                      X, ALU.max, negate=True).then_inc(S["nmax_ready"], 1)
                yield 17.2
                dve.wait_ge(S["pe_ready"], B * G)
                dve.reciprocal(inv_sum[:, :], psum_r[:, :]).then_inc(S["inv_ready"], 1)
                if late:
                    yield from take_over((18.2, 18.4))
                for h in range(HG):
                    yield (19.8, 20.2, 20.4, 20.8)[h]
                    dve.wait_ge(S["inv_ready"], 1)
                    dve.wait_ge(S["pv_ps"], G)
                    o = ao_m[:, :, :, h * HD:(h + 1) * HD].rearrange("p b g d -> p (b g) d")
                    s_ = b4[:, :].rearrange("p (n f) -> p n f", f=32)[:, :, h * HD:(h + 1) * HD]
                    dve.scalar_tensor_tensor(o, s_, part("cst", "head_p", h, 1), bcast(inv_sum[:, :], 2, [P, 16, HD]),
                                             ALU.mult, ALU.mult).then_inc(S["aom_ready"], 1)
                yield 21.8
                dve.wait_ge(S["wo_ps"], 1)
                dve.wait_ge(S["x3c_ready"], 1)
                dve.tensor_tensor(x3[:, M_ZERO:], x3[:, M_ZERO:], b3[:, M_ZERO:P], ALU.add).then_inc(S["x3_ready"], 1)
                dve.wait_ge(S["base_ready"], 1)
                dve.tensor_tensor(base[:, M_ZERO:], base[:, M_ZERO:], b3[:, M_ZERO:P], ALU.add).then_inc(S["base_ready"], 1)
                yield 22.2
                dve.wait_ge(S["x3_ready"], 1)
                step(dve.scalar_tensor_tensor(sq2[:, :], x3[:, :], 1.0, x3[:, :], ALU.mult, ALU.mult,
                                              accum_out=rs2[:, 3:4]))
                yield 22.4
                after()
                dve.tensor_scalar(rs2[:, 4:5], rs2[:, 3:4], 1.0 / D, EPS, ALU.mult, ALU.add).then_inc(S["ms2_ready"], 1)
                yield 23.4
                dve.wait_ge(S["r2_ready"], 1)
                dve.tensor_scalar(xn[:, :], x3[:, :], rs2[:, 5:6], None, ALU.mult).then_inc(S["xn_ready"], 1)

            def mixture(banks=(b2, b3, b4), apart=False):
                step, after = chained("dchain3")
                ba, bb, bc = banks

                def swiglu(j, at):
                    yield at[0]
                    dve.wait_ge(S["e1_th"], j + 1)
                    dve.scalar_tensor_tensor(e_a[:, j, :], th_e[:, j, :], 1.0, bc[:, 0:P], ALU.add,
                                             ALU.mult).then_inc(S["ea_ready"], 1)
                    yield at[1]
                    dve.wait_ge(S["ea_ready"], j + 1)
                    dve.tensor_tensor(e_h[:, j, :], e_a[:, j, :], bc[:, P:2 * P], ALU.mult).then_inc(S["eh_ready"], 1)

                lg, eq, clean, d, e_, mx, first, mask, q = (sm2[:, 8 * k:8 * k + 8] for k in range(9))
                cols = slice(0, E2)
                yield 24.2
                step(dve.memset(clean[:, cols], 0.0))
                step(dve.memset(e_, -1.0))
                yield 24.4
                dve.wait_ge(S["gt_ps"], 1)
                dve.tensor_copy(lg[:, cols], bc[:, 0:E2]).then_inc(S["ge_nl"], 1)
                yield 24.8
                dve.wait_ge(S["ge_nl"], 1)
                step(dve.tensor_tensor(eq.bitcast(U32)[:, cols], lg[:, cols], lg[:, cols], ALU.is_equal))
                yield 25.2
                after()
                step(dve.copy_predicated(clean[:, cols], eq.bitcast(U32)[:, cols], lg[:, cols]))
                yield from swiglu(0, (25.4, 25.8))
                after()
                step(dve.tensor_scalar(clean[:, cols], clean[:, cols], FLT_MAX, -FLT_MAX, ALU.min, ALU.max))
                yield 26.2
                after()
                step(dve.tensor_reduce(q[:, 0:1], clean[:, cols], X, ALU.max))
                yield 26.4
                after()
                dve.tensor_scalar(d[:, cols], clean[:, cols], q[:, 0:1], None, ALU.subtract).then_inc(S["ge_e"], 1)
                yield from swiglu(1, (26.8, 27.2))
                yield 27.4
                dve.wait_ge(S["e_ready"], 1)
                step(dve.max(mx, e_))
                step(dve.tensor_reduce(q[:, 1:2], e_[:, cols], X, ALU.add))
                yield 27.8
                after()
                step(dve.max_index(ix2[:, :], mx, e_))
                step(dve.tensor_tensor(q[:, 2:3], mx[:, 0:1], mx[:, 1:2], ALU.add))
                yield 28.2
                after()
                step(dve.tensor_scalar(first, count8, ix2[:, 0:1], None, ALU.is_equal))
                step(dve.scalar_tensor_tensor(q[:, 3:4], q[:, 1:2], 1e-8, q[:, 2:3], ALU.mult, ALU.add))
                yield 28.4
                after()
                step(dve.scalar_tensor_tensor(mask, count8, ix2[:, 1:2], first, ALU.is_equal, ALU.add))
                step(dve.reciprocal(q[:, 4:5], q[:, 3:4]))
                yield 28.8
                after()
                step(dve.scalar_tensor_tensor(wts[:, :], mask, q[:, 4:5], e_, ALU.mult, ALU.mult))
                if not apart:
                    dve.wait_ge(S["base_ready"], 2)
                dve.wait_ge(S["fin_free"], 1)
                step(dve.tensor_copy(fin[:, 0:M_ZERO], base[:, 0:M_ZERO]))
                yield 29.2
                after()
                step(dve.tensor_scalar(q[:, 5:6], wts[:, 1:2], 0.5, None, ALU.mult))
                w_of = (wts[:, 0:1], q[:, 5:6], wts[:, 3:4], wts[:, 2:3])
                for k, bk in enumerate((bc, bb, ba, bc)):
                    yield (29.4, 29.8, 30.2, 30.4)[k]
                    dve.wait_ge(S["o_ps"], k + 1)
                    if k == 0:
                        after()
                    else:
                        dve.wait_ge(S["moe_ready"], k)
                    dve.scalar_tensor_tensor((fin if k == E2 - 1 else base)[:, M_ZERO:], bk[:, M_ZERO:P], w_of[k],
                                             base[:, M_ZERO:], ALU.mult, ALU.add).then_inc(S["moe_ready"], 1)

            dve.memset(idle[:, :], 0.0).then_inc(idle_ready, 1)
            dve.memset(h2[:, :, :], 0.0).then_inc(dve_setup, 1)
            dve.memset(run[:, :, :], 0.0).then_inc(dve_setup, 1)
            dve.memset(x_sb[:, NC * P:], 0.0).then_inc(dve_setup, 1)
            dve.wait_ge(in_rec, 3 * 16)
            dve.wait_ge(rec_ps, 1)
            for gate in range(3):
                dve.tensor_scalar(gate_bias[:, gate, :], b0[:, gate * B:(gate + 1) * B],
                                  part("vec", ("b_z", "b_r", "b")[gate]), None, ALU.add).then_inc(gb_ready, 1)
            for gate, (name, f) in enumerate((("U_z", 0.5), ("U_r", 0.5), ("U", 0.25), ("U_r", -0.25))):
                dve.tensor_scalar(u_half[:, gate, :], part("rec", name), f, None, ALU.mult).then_inc(u_ready, 1)
            dve.wait_ge(dve_setup, 3)
            dve.tensor_copy(cond_rep[:, :, :], bcast(part("vec", "cond"), 2, [P, B, TC])).then_inc(cr_ready, 1)
            dve.wait_ge(cr_ready, 1)
            dve.tensor_copy(mask_bf[:, :], part("cst", "mask")).then_inc(u_ready, 1)
            dve.tensor_copy(ident_bf[:, :], ident).then_inc(dve_setup, 1)
            dve.tensor_tensor(sm[:, 0:HD], part("vec", "qn"), part("vec", "kn"), ALU.mult).then_inc(dve_setup, 1)
            dve.wait_ge(dve_setup, 5)
            dve.tensor_scalar(sm[:, 8:16], sm[:, 0:HD], HD ** -0.5, None, ALU.mult).then_inc(dve_setup, 1)
            dve.wait_ge(dve_setup, 6)
            dve.tensor_copy(qk_scale[:, :].rearrange("p (h d) -> p h d", d=HD), bcast(sm[:, 8:16], 1, [P, HEADS, HD])).then_inc(dve_setup, 1)

            def one_pass(c, R, before, nk):
                if nk:
                    gru(pacer(part1(c - 1, before), attention(c - 2, nk), mixture()), c, R, before)
                else:
                    gru(pacer(part1(0, before, alone=True) if before else setup()), c, R, before)
            chunks(dve, "dve", one_pass)
            begin(dve, "dve", parts_go, NC)
            merge(part1(NC - 1, R[1]), attention(NC - 2, NC))
            dve.drain().then_inc(S["parts_done"], 1)
            begin(dve, "dve", parts_go, NC + 1)
            merge(earlier(mixture((b0, bk_z, bk_r), apart=True), 23), attention(NC - 1, NC, late=True))
            dve.drain().then_inc(S["parts_done"], 1)
            begin(dve, "dve", parts_go, NC + 2)
            merge(earlier(mixture(apart=True), 23))

        @block.gpsimd
        def _(pool):
            def heads_of_q():
                for h in range(0, HEADS, HG):
                    pool.tensor_tensor(q_m[:, :, h:h + HG, :], bcast(q_f[:, :, :], 2, [P, B, HG, TC]),
                                       part("cst", "head_f", h, HG).unsqueeze(1).unsqueeze(3)
                                       .to_broadcast([P, B, HG, TC]), ALU.mult).then_inc(S["qm_ready"], 1)

            def sigmoid_e():
                pool.wait_ge(S["nl_ready"], 1)
                pool.tensor_tensor(sm[:, 8:16], e_const[:, :], sm[:, 0:8], ALU.pow).then_inc(S["sig_e"], 1)

            def part1():
                pool.wait_ge(S["ms_ready"], 1)
                pool.tensor_tensor(rs[:, 2:3], rs[:, 1:2], neg_half[:, 0:1], ALU.pow).then_inc(S["r1_ready"], 1)
                pool.wait_ge(S["ssh_ready"], 1)
                pool.tensor_tensor(r_h[:, :], ss_h[:, :], neg_half[:, :], ALU.pow).then_inc(S["rh_ready"], 1)

            def norm2():
                pool.wait_ge(S["ms2_ready"], 1)
                pool.tensor_tensor(rs2[:, 5:6], rs2[:, 4:5], neg_half[:, 0:1], ALU.pow).then_inc(S["r2_ready"], 1)

            def gate_e():
                pool.wait_ge(S["ge_e"], 1)
                pool.tensor_tensor(sm2[:, 32:32 + E2], e_const[:, 0:E2], sm2[:, 24:24 + E2],
                                   ALU.pow).then_inc(S["e_ready"], 1)

            def next_parts():
                pool.wait_ge(S["parts_done"], 4)
                pool.sem_clear(span(S))
                pool.drain().then_inc(parts_go, 1)

            def clear(before):
                pool.wait_ge(before["left"], 3)
                pool.sem_clear(span(before))
                pool.drain().then_inc(cleared, 1)

            pool.memset(e_const[:, :], 2.718281828459045)
            pool.memset(neg_half[:, :], -0.5)
            pool.memset(v_c[:, :], 0.0)
            pool.memset(k_c[:, :], 0.0).then_inc(pool_setup, 1)
            pool.wait_ge(pool_setup, 1)
            next_parts()
            clear(R[0])
            sigmoid_e()
            part1()
            next_parts()
            with pool.Fori(2, NC - 1, 2):
                for k in range(2):
                    clear(R[1 - k])
                    sigmoid_e()
                    heads_of_q()
                    part1()
                    norm2()
                    gate_e()
                    next_parts()
            heads_of_q()
            sigmoid_e()
            part1()
            norm2()
            next_parts()
            heads_of_q()
            gate_e()
            norm2()
            next_parts()
            gate_e()

        @block.sync
        def _(sp):
            sp.dma_start(packs["rec"][0][:, :], rec[:, :]).then_inc(in_rec, 16)
            sp.dma_start(packs["vec"][0][:, :], vec[:, :]).then_inc(in_rec, 16)
            sp.dma_start(packs["cst"][0][:, :], cst[:, :]).then_inc(in_rec, 16)
            sp.dma_start(x_sb[:, 0:NC * P], xT[:, :]).then_inc(in_x, 16)
            sp.dma_start(packs["mix"][0][:, :], mix[:, :]).then_inc(in_mix, 16)
            sp.dma_start(packs["ffn"][0][:, :], ffn[:, :]).then_inc(in_ffn, 16)
            sp.wait_ge(in_mix, 16)
            sp.wait_ge(in_ffn, 16)
            sp.sem_inc(S["parts_done"], 1)
            begin(sp, "sp", parts_go, 1)
            sp.sem_inc(S["parts_done"], 1)

            def store(tile):
                sp.sem_inc(S["fin_free"], 1)
                sp.wait_ge(S["moe_ready"], E2)
                sp.dma_start(out[bass.ds(tile, 1), :, :].rearrange("a p f -> (a p) f"), fin[:, :]).then_inc(out_done, 16)

            begin(sp, "sp", parts_go, 2)
            store(0)
            sp.sem_inc(S["parts_done"], 1)
            with sp.Fori(3, NC) as c:
                begin(sp, "sp", parts_go, c)
                sp.wait_ge(out_done, 16 * (c - 2))
                store(c - 2)
                sp.sem_inc(S["parts_done"], 1)
            begin(sp, "sp", parts_go, NC)
            sp.sem_inc(S["parts_done"], 1)
            for tile in (NC - 2, NC - 1):
                begin(sp, "sp", parts_go, tile + 3)
                sp.wait_ge(out_done, 16 * tile)
                store(tile)
                if tile == NC - 2:
                    sp.sem_inc(S["parts_done"], 1)
            sp.wait_ge(out_done, 16 * NC)


def constants():
    import numpy as np
    p = np.arange(P)[:, None]
    t = np.arange(TC)[None, :]
    inv = np.broadcast_to(0.5 / (np.arange(T) + 1.0), (P, T))
    mask = np.where(np.arange((2 * NC - 1) * TC)[None, :] - (NC - 1) * TC <= p % TC, 0.0, NEG)
    made = {"ident": np.eye(P), "inv": inv, "head_f": p // HD == np.arange(HEADS)[None, :],
            "head_p": p // TC == np.arange(HG)[None, :], "pick_t": p % TC == t,
            "count8": np.broadcast_to(np.arange(8), (P, 8)), "mask": mask}
    return np.concatenate([np.asarray(made[n], np.float32).reshape(P, w) for n, w in CST], axis=1)


def kernel(**inputs):
    import numpy as np
    import concourse.bacc as bacc
    from concourse import mybir as mb
    from concourse.bass_utils import run_bass_kernel_spmd as run_spmd

    a = {n: np.asarray(v) for n, v in inputs.items()}

    def rows(w):
        return np.concatenate(np.split(w, w.shape[0] // P, axis=0), axis=1)

    def square(w):
        return np.concatenate([w[k * P:(k + 1) * P, j * P:(j + 1) * P] for j in range(2) for k in range(2)], axis=1)

    col = lambda v: v.reshape(P, 1)
    wide = lambda v: np.broadcast_to(v, (P, v.shape[0]))
    c, m, f = "L0_cond_", "L0_cond2_", "L0_ffn_"
    rec = [a[c + n] for n, _ in REC]
    vec = [col(a[c + "b_z"]), col(a[c + "b_r"]), col(a[c + "b"]), col(a[f + "n1_w"]), col(a[f + "n2_w"]),
           a["cond_1024"].T, wide(a[m + "router_bias"]), wide(a[f + "qn_w"]), wide(a[f + "kn_w"])]
    mix = [a[m + "router_W"][:P], a[m + "router_W"][P:], a[m + "w1"], a[m + "w3"], rows(a[m + "w2"]),
           *a[m + "W1e"], *a[m + "W2e"]]
    ffn = [a[f + "wq"].T, a[f + "wk"].T, a[f + "wv"].T, a[f + "wo"].T,
           a[f + "gate_w"].T, a[f + "e0_up"].T, a[f + "e1_w1"].T, a[f + "e1_w2"].T, a[f + "e2_l1"].T, a[f + "e3_down"].T,
           rows(a[f + "e0_down"].T), rows(a[f + "e1_down"].T), square(a[f + "e2_l2"].T), square(a[f + "e2_l3"].T),
           rows(a[f + "e2_l4"].T), a[f + "e3_up"].T, rows(a[f + "e3_out"].T)]
    x = a["x"].reshape(B, NC, TC, D).transpose(3, 1, 0, 2).reshape(D, NC * P)
    arrays = {"xT": x, "rec": np.concatenate(rec, 1), "vec": np.concatenate(vec, 1), "cst": constants(),
              "mix": np.concatenate(mix, 1), "ffn": np.concatenate(ffn, 1)}
    arrays = {n: np.ascontiguousarray(v) for n, v in arrays.items()}

    nc = bacc.Bacc("TRN2", target_bir_lowering=False, num_devices=1)
    aps = [nc.dram_tensor(n, v.shape, mb.dt.float32, kind="ExternalInput").ap() for n, v in arrays.items()]
    out = nc.dram_tensor("out", (NC, P, D), mb.dt.float32, kind="ExternalOutput").ap()
    build(nc, *aps, out)
    got = run_spmd(nc, [arrays], core_ids=[0]).results[0]["out"]
    return got.reshape(NC, B, TC, D).transpose(1, 0, 2, 3).reshape(B, T, D)
```
